# Optimizing a Trainium2 kernel written in Bass

```python
import numpy as np
import jax
import jax.numpy as jnp

def _softmax(x, axis=-1):
    return jax.nn.softmax(x, axis=axis)

def _gelu(x):
    return jax.nn.gelu(x, approximate=True)

def _silu(x):
    return jax.nn.silu(x)

def _sigmoid(x):
    return jax.nn.sigmoid(x)

def _layernorm(x, axis=-1, eps=1e-05):
    m = jnp.mean(x, axis=axis, keepdims=True)
    v = jnp.var(x, axis=axis, keepdims=True)
    return (x - m) / jnp.sqrt(v + eps)

def _scatter_add(tgt, idx, src, axis=0):
    return tgt.at[idx].add(src)

def _segment_sum(src, seg, n):
    return jax.ops.segment_sum(src, seg, n)
kernel_name = 'mk_gnn_resnorm_d4_gnn_r32_9f77a1'

def setup_inputs(seed: int=0):
    np.random.seed(seed)
    _w = jnp.asarray

    def _rec_inputs():
        import jax
        import jax.numpy as jnp
        _gk = jax.random.key(seed)
        x = -0.0003713 + 1 * jax.random.normal(jax.random.fold_in(_gk, 1), (50000, 256), jnp.float32)
        src = jax.random.randint(jax.random.fold_in(_gk, 2), (25000,), 0, 50000, jnp.int32)
        dst = jax.random.randint(jax.random.fold_in(_gk, 3), (25000,), 0, 50000, jnp.int32)
        _o = jnp.argsort(dst, stable=True)
        src = src[_o]
        dst = dst[_o]
        edge_attr_16 = 0.000254156 + 0.999948 * jax.random.normal(jax.random.fold_in(_gk, 12), (25000, 16), jnp.float32)
        edge_weight = jax.random.uniform(jax.random.fold_in(_gk, 14), (25000,), jnp.float32, 0.0, 1)
        return (x, src, dst, edge_attr_16, edge_weight)
    x, src, dst, edge_attr_16, edge_weight = _rec_inputs()

    def _L0_gnn_setup():
        import jax, jax.numpy as jnp
        import numpy as np
        N_NODES = 50000
        N_EDGES = 25000
        N_FEAT = 256
        N_CLASSES = 256
        K_HOPS = 2
        key = jax.random.key(seed)
        k1, k2, k3 = jax.random.split(key, 3)
        x = jax.random.normal(k1, (N_NODES, N_FEAT), dtype=jnp.float32)
        edge_index = jax.random.randint(k2, (2, N_EDGES), 0, N_NODES, dtype=jnp.int32)
        W = jax.random.normal(k3, (N_CLASSES, N_FEAT), dtype=jnp.float32) * 0.05
        b = jnp.zeros((N_CLASSES,), dtype=jnp.float32)
        return {'x': x, 'edge_index': edge_index, 'W': W, 'b': b}
    _L0_gnn_all = _L0_gnn_setup()
    _L0_gnn_in = {k: v for k, v in _L0_gnn_all.items() if k in ('W', 'b')}
    del _L0_gnn_all

    def _L1_gnn_setup():
        import jax, jax.numpy as jnp
        import numpy as np
        N_NODES = 3125
        N_EDGES = 100000
        NFEAT = 256
        NHID = 256
        key = jax.random.key(seed)
        k_x, k_ws, k_wn, k_src, k_dst = jax.random.split(key, 5)
        x = jax.random.normal(k_x, (N_NODES, NFEAT), dtype=jnp.float32)
        W_self = jax.random.normal(k_ws, (NFEAT, NHID), dtype=jnp.float32) * (1.0 / np.sqrt(NFEAT))
        W_neigh = jax.random.normal(k_wn, (NFEAT, NHID), dtype=jnp.float32) * (1.0 / np.sqrt(NFEAT))
        b = jnp.zeros((NHID,), dtype=jnp.float32)
        edge_src = jax.random.randint(k_src, (N_EDGES,), 0, N_NODES, dtype=jnp.int32)
        edge_dst = jax.random.randint(k_dst, (N_EDGES,), 0, N_NODES, dtype=jnp.int32)
        return {'x': x, 'W_self': W_self, 'W_neigh': W_neigh, 'b': b, 'edge_src': edge_src, 'edge_dst': edge_dst}
    _L1_gnn_all = _L1_gnn_setup()
    _L1_gnn_in = {k: v for k, v in _L1_gnn_all.items() if k in ('W_self', 'W_neigh', 'b')}
    del _L1_gnn_all

    def _L2_gnn_setup():
        import jax, jax.numpy as jnp
        import numpy as np
        N, D, H = (50000, 256, 8)
        HD = D // H
        E = 25000
        NEG_SLOPE = 0.2

        def _gat_layer(x, edge_index, W, att_src, att_dst, bias, ln_g, ln_b, W1, b1, W2, b2):
            n = x.shape[0]
            sl = jnp.arange(n, dtype=edge_index.dtype)
            src = jnp.concatenate([edge_index[0], sl])
            dst = jnp.concatenate([edge_index[1], sl])
            xp = (x @ W).reshape(n, H, HD)
            a_src = jnp.einsum('nhd,hd->nh', xp, att_src)
            a_dst = jnp.einsum('nhd,hd->nh', xp, att_dst)
            e = a_src[src] + a_dst[dst]
            e = jax.nn.leaky_relu(e, NEG_SLOPE)
            m = jax.ops.segment_max(e, dst, num_segments=n)
            ex = jnp.exp(e - m[dst])
            denom = jax.ops.segment_sum(ex, dst, num_segments=n)
            alpha = ex / (denom[dst] + 1e-16)
            msg = alpha[:, :, None] * xp[src]
            out = jax.ops.segment_sum(msg, dst, num_segments=n)
            h = out.reshape(n, D) + bias
            r = h + x
            mu = jnp.mean(r, axis=-1, keepdims=True)
            var = jnp.mean(jnp.square(r - mu), axis=-1, keepdims=True)
            hn = (r - mu) / jnp.sqrt(var + 1e-05) * ln_g + ln_b
            return jax.nn.relu(hn @ W1 + b1) @ W2 + b2
        key = jax.random.key(seed)
        ks = jax.random.split(key, 12)
        s = 1.0 / np.sqrt(D)
        return {'x': jax.random.normal(ks[0], (N, D), jnp.float32), 'edge_index': jax.random.randint(ks[1], (2, E), 0, N, jnp.int64), 'edge_attr': jax.random.normal(ks[2], (E, 16), jnp.float32), 'W': jax.random.normal(ks[3], (D, D), jnp.float32) * s, 'att_src': jax.random.normal(ks[4], (H, HD), jnp.float32) * s, 'att_dst': jax.random.normal(ks[5], (H, HD), jnp.float32) * s, 'bias': jnp.zeros((D,), jnp.float32), 'ln_g': jnp.ones((D,), jnp.float32), 'ln_b': jnp.zeros((D,), jnp.float32), 'W1': jax.random.normal(ks[6], (D, D), jnp.float32) * s, 'b1': jnp.zeros((D,), jnp.float32), 'W2': jax.random.normal(ks[7], (D, D), jnp.float32) * s, 'b2': jnp.zeros((D,), jnp.float32)}
    _L2_gnn_all = _L2_gnn_setup()
    _L2_gnn_in = {k: v for k, v in _L2_gnn_all.items() if k in ('W', 'att_src', 'att_dst', 'bias', 'ln_g', 'ln_b', 'W1', 'b1', 'W2', 'b2')}
    del _L2_gnn_all

    def _L3_gnn_setup():
        import jax, jax.numpy as jnp
        import numpy as np
        N_NODES = 3125
        N_EDGES = 100000
        D_IN = 256
        D_OUT = 256
        key = jax.random.key(seed)
        k1, k2, k3, k4, k5 = jax.random.split(key, 5)
        x = jax.random.normal(k1, (N_NODES, D_IN), dtype=jnp.float32)
        edge_index = jax.random.randint(k2, (2, N_EDGES), 0, N_NODES, dtype=jnp.int32)
        edge_weight = jax.random.uniform(k3, (N_EDGES,), dtype=jnp.float32)
        limit = float(np.sqrt(6.0 / (D_IN + D_OUT)))
        weight = jax.random.uniform(k4, (D_IN, D_OUT), dtype=jnp.float32, minval=-limit, maxval=limit)
        bias = jax.random.normal(k5, (D_OUT,), dtype=jnp.float32) * 0.01
        return {'x': x, 'edge_index': edge_index, 'edge_weight': edge_weight, 'weight': weight, 'bias': bias}
    _L3_gnn_all = _L3_gnn_setup()
    _L3_gnn_in = {k: v for k, v in _L3_gnn_all.items() if k in ('weight', 'bias')}
    del _L3_gnn_all
    return {'x': x, 'src': src, 'dst': dst, 'edge_attr_16': edge_attr_16, 'edge_weight': edge_weight, 'L0_gnn_W': _L0_gnn_in['W'], 'L0_gnn_b': _L0_gnn_in['b'], 'L1_gnn_W_self': _L1_gnn_in['W_self'], 'L1_gnn_W_neigh': _L1_gnn_in['W_neigh'], 'L1_gnn_b': _L1_gnn_in['b'], 'L2_gnn_W': _L2_gnn_in['W'], 'L2_gnn_att_src': _L2_gnn_in['att_src'], 'L2_gnn_att_dst': _L2_gnn_in['att_dst'], 'L2_gnn_bias': _L2_gnn_in['bias'], 'L2_gnn_ln_g': _L2_gnn_in['ln_g'], 'L2_gnn_ln_b': _L2_gnn_in['ln_b'], 'L2_gnn_W1': _L2_gnn_in['W1'], 'L2_gnn_b1': _L2_gnn_in['b1'], 'L2_gnn_W2': _L2_gnn_in['W2'], 'L2_gnn_b2': _L2_gnn_in['b2'], 'L3_gnn_weight': _L3_gnn_in['weight'], 'L3_gnn_bias': _L3_gnn_in['bias']}

def reference(x, src, dst, edge_attr_16, edge_weight, L0_gnn_W, L0_gnn_b, L1_gnn_W_self, L1_gnn_W_neigh, L1_gnn_b, L2_gnn_W, L2_gnn_att_src, L2_gnn_att_dst, L2_gnn_bias, L2_gnn_ln_g, L2_gnn_ln_b, L2_gnn_W1, L2_gnn_b1, L2_gnn_W2, L2_gnn_b2, L3_gnn_weight, L3_gnn_bias):
    import jax
    import jax.numpy as jnp

    def _L0_gnn_ref(x, edge_index, W, b):
        import jax, jax.numpy as jnp
        import numpy as np
        N_NODES = 50000
        N_EDGES = 25000
        N_FEAT = 256
        N_CLASSES = 256
        K_HOPS = 2
        n = x.shape[0]
        loop = jnp.arange(n, dtype=edge_index.dtype)
        row = jnp.concatenate([edge_index[0], loop])
        col = jnp.concatenate([edge_index[1], loop])
        deg = jax.ops.segment_sum(jnp.ones_like(col, dtype=x.dtype), col, num_segments=n)
        dinv = jnp.where(deg > 0, jax.lax.rsqrt(deg), jnp.zeros_like(deg))
        norm = dinv[row] * dinv[col]

        def hop(h, _):
            msg = h[row] * norm[:, None]
            h_new = jax.ops.segment_sum(msg, col, num_segments=n)
            return (h_new, None)
        h, _ = jax.lax.scan(hop, x, None, length=K_HOPS)
        logits = h @ W.T + b
        return jax.nn.log_softmax(logits, axis=1)

    def _L1_gnn_ref(x, W_self, W_neigh, b, edge_src, edge_dst):
        import jax, jax.numpy as jnp
        import numpy as np
        N_NODES = 3125
        N_EDGES = 100000
        NFEAT = 256
        NHID = 256
        n = x.shape[0]
        msg = x[edge_src]
        agg = jax.ops.segment_sum(msg, edge_dst, num_segments=n)
        deg = jax.ops.segment_sum(jnp.ones_like(edge_dst, dtype=x.dtype), edge_dst, num_segments=n)
        h_neigh = agg / jnp.maximum(deg, 1.0)[:, None]
        out = x @ W_self + h_neigh @ W_neigh + b
        return jax.nn.relu(out)

    def _L2_gnn_ref(x, edge_index, edge_attr, W, att_src, att_dst, bias, ln_g, ln_b, W1, b1, W2, b2):
        import jax, jax.numpy as jnp
        import numpy as np
        N, D, H = (50000, 256, 8)
        HD = D // H
        E = 25000
        NEG_SLOPE = 0.2

        def _gat_layer(x, edge_index, W, att_src, att_dst, bias, ln_g, ln_b, W1, b1, W2, b2):
            n = x.shape[0]
            sl = jnp.arange(n, dtype=edge_index.dtype)
            src = jnp.concatenate([edge_index[0], sl])
            dst = jnp.concatenate([edge_index[1], sl])
            xp = (x @ W).reshape(n, H, HD)
            a_src = jnp.einsum('nhd,hd->nh', xp, att_src)
            a_dst = jnp.einsum('nhd,hd->nh', xp, att_dst)
            e = a_src[src] + a_dst[dst]
            e = jax.nn.leaky_relu(e, NEG_SLOPE)
            m = jax.ops.segment_max(e, dst, num_segments=n)
            ex = jnp.exp(e - m[dst])
            denom = jax.ops.segment_sum(ex, dst, num_segments=n)
            alpha = ex / (denom[dst] + 1e-16)
            msg = alpha[:, :, None] * xp[src]
            out = jax.ops.segment_sum(msg, dst, num_segments=n)
            h = out.reshape(n, D) + bias
            r = h + x
            mu = jnp.mean(r, axis=-1, keepdims=True)
            var = jnp.mean(jnp.square(r - mu), axis=-1, keepdims=True)
            hn = (r - mu) / jnp.sqrt(var + 1e-05) * ln_g + ln_b
            return jax.nn.relu(hn @ W1 + b1) @ W2 + b2
        return _gat_layer(x, edge_index, W, att_src, att_dst, bias, ln_g, ln_b, W1, b1, W2, b2)

    def _L3_gnn_ref(x, edge_index, edge_weight, weight, bias):
        import jax, jax.numpy as jnp
        import numpy as np
        N_NODES = 3125
        N_EDGES = 100000
        D_IN = 256
        D_OUT = 256
        support = x @ weight
        row, col = (edge_index[0], edge_index[1])
        msgs = support[col] * edge_weight[:, None]
        out = jax.ops.segment_sum(msgs, row, num_segments=x.shape[0])
        return out + bias
    edge_index = jnp.stack([src, dst])
    x = _layernorm(x + _L0_gnn_ref(x, edge_index, L0_gnn_W, L0_gnn_b), axis=-1)
    x = _layernorm(x + _L1_gnn_ref(x, L1_gnn_W_self, L1_gnn_W_neigh, L1_gnn_b, src, dst), axis=-1)
    x = _layernorm(x + _L2_gnn_ref(x, edge_index, edge_attr_16, L2_gnn_W, L2_gnn_att_src, L2_gnn_att_dst, L2_gnn_bias, L2_gnn_ln_g, L2_gnn_ln_b, L2_gnn_W1, L2_gnn_b1, L2_gnn_W2, L2_gnn_b2), axis=-1)
    x = _layernorm(x + _L3_gnn_ref(x, edge_index, edge_weight, L3_gnn_weight, L3_gnn_bias), axis=-1)
    return x

_drawn_inputs = setup_inputs


def setup_inputs(seed=0):
    import zlib

    import numpy as np

    out = dict(_drawn_inputs(seed))
    spreads = {'L0_gnn_b': (0.0, 0.1),
     'L1_gnn_b': (0.0, 0.1),
     'L2_gnn_bias': (0.0, 0.1),
     'L2_gnn_ln_g': (1.0, 0.2),
     'L2_gnn_ln_b': (0.0, 0.1),
     'L2_gnn_b1': (0.0, 0.1),
     'L2_gnn_b2': (0.0, 0.1)}
    factors = {'L2_gnn_att_dst': 5.999, 'L3_gnn_bias': 6.147}
    for name, (base, spread) in spreads.items():
        noise = np.random.default_rng([zlib.crc32(name.encode()), seed]).standard_normal(out[name].shape)
        drawn = base * np.exp(spread * noise) if base else spread * noise
        out[name] = jnp.asarray(drawn.astype(out[name].dtype))
    for name, factor in factors.items():
        out[name] = (out[name] * factor).astype(out[name].dtype)
    return out
```

```python
import concourse.bass as bass
from concourse import mybir
from contextlib import ExitStack

F32 = mybir.dt.float32
BF16 = mybir.dt.bfloat16
I32 = mybir.dt.int32
ALU = mybir.AluOpType
ACT = mybir.ActivationFunctionType
AXX = mybir.AxisListType.X

P = 128
N = 50000
E = 25000
D = 256
HEADS = 8
HD = D // HEADS
RADIX = 256
HIGH = -(-N // RADIX)
NPAD = HIGH * RADIX
PAD = NPAD - 1

J = 2
GROUP = J * P
NG = NPAD // GROUP
LAST = (N - (NG - 1) * GROUP) // J
U = 4

IC = -(-E // P)
IH = IC // 2
EC = P - 1
NC = 200
BIG = 1.0e30
FAR = 1 << 20
XW = D + 2 * HEADS


def rounds(eng, n, stages, u=U, lead=None, peel=False):
    deep = max(lag for lag, _ in stages)
    lead = lead or u * (1 + -(-max(deep, 1) // u))
    end = n // u * u - (u if peel else 0)

    def step(i):
        for lag, f in stages:
            g = i - lag
            if 0 <= g < n:
                f(g, g % u, g // u)

    for i in range(lead):
        step(i)
    with eng.Fori(lead // u, end // u) as r:
        for k in range(u):
            for lag, f in stages:
                c = k - lag
                f(r * u + c, c % u, r + c // u)
    for i in range(end, n + deep):
        step(i)


def started(g, n=U):
    return not isinstance(g, int) or g >= n


class Count:

    def __init__(self, sem, per=1, total=0):
        self.sem, self.per, self.total = sem, per, total

    def at(self, g, k=None, run=0):
        return g * self.per + (run * self.total * self.per + (self.per if k is None else k))


def gnn_program(nc, x, src, dst, edge_weight, W0, b0, Wself, Wneigh, b1, Wg, att_src, att_dst,
                gat_bias, ln_g, ln_b, Wm1, bm1, Wm2, bm2, Wl3, bl3, out, dbg=None):
    ctx = ExitStack()
    with ctx:
        def sem(name):
            return ctx.enter_context(nc.semaphore(name))

        def sb(name, shape, dt=F32, where=ctx):
            return where.enter_context(nc.sbuf_tensor(name, shape, dt))

        def pb(name, shape, where=ctx):
            return where.enter_context(nc.psum_tensor(name, shape, F32))

        ident = sb("ident", [P, P])
        flip = sb("flip", [P, P])
        ones_f = sb("ones_f", [P, P])
        ones_b = sb("ones_b", [P, P], BF16)
        before = sb("before", [P, P], BF16)
        upto = sb("upto", [P, P], BF16)
        counting = sb("counting", [P, RADIX], BF16)
        zero_w = sb("zero_w", [1, XW])
        not0 = sb("not0", [P, 1])
        is0 = sb("is0", [P, 1])
        neg0 = sb("neg0", [P, 1])

        at = [sb(f"at{o}", [P, NC, 3], I32) for o in range(2)]
        key_in = [sb(f"key_in{o}", [P, NC]) for o in range(2)]
        key_out = [sb(f"key_out{o}", [P, NC]) for o in range(2)]
        weight = sb("weight", [P, NC])
        gate_fwd = sb("gate_fwd", [P, NC])
        gate_bwd = sb("gate_bwd", [P, NC])
        first = sb("first", [P, NC])
        diag = sb("diag", [P, 2, 4, P])
        same = sb("same", [P, NC, P], BF16)
        dinv = sb("dinv", [P, NG, J])
        dinv2 = sb("dinv2", [P, NG, J])
        rdeg = sb("rdeg", [P, NG, J])
        has_in = sb("has_in", [P, NG, J])

        def table(name, shape):
            return nc.dram_tensor(name, shape, F32, kind="Internal").ap()

        deg_tab = table("deg_tab", (NPAD, 1))
        dinv_tab = table("dinv_tab", (NPAD, 1))
        sums = table("sums", (NPAD, D))
        sums_gat = table("sums_gat", (NPAD, XW))
        sums_src = table("sums_src", (NPAD, D))
        y1 = table("y1", (NPAD, D))
        x1 = table("x1", (NPAD, D))
        x2 = table("x2", (NPAD, D))
        x3 = table("x3", (NPAD, D))
        xp = table("xp", (NPAD, D))
        a16 = table("a16", (NPAD, 2 * HEADS))
        bank = [pb(f"bank{i}", [P, 512]) for i in range(8)]

        def square(name, t=2, w=D):
            return sb(name, [P, t, w])
        w0t, w_self, w_neigh, w_gat, w_m1, w_m2, w_l3 = (
            square(n) for n in ("w0t", "w_self", "w_neigh", "w_gat", "w_m1", "w_m2", "w_l3"))
        w_att = square("w_att", 2, 2 * HEADS)
        rows = {n: sb(n, [P, D]) for n in ("b0_row", "b1_row", "gat_row", "m2_row", "l3_row")}
        b0_row, b1_row, gat_row, m2_row, l3_row = rows.values()
        m1_col = sb("m1_col", [P, 2])
        eps = sb("eps", [P, 1])

        tmp = ExitStack()
        raw = [sb(f"raw{a}", [IH, 2, P], I32, tmp) for a in range(2)]
        raw_w = sb("raw_w", [IH, 2, P], F32, tmp)
        digit_i = sb("digit_i", [IH, 4, 2, P], I32, tmp)
        digit_f = sb("digit_f", [IH, 4, 2, P], F32, tmp)
        part = sb("part", [P, 7, IC], F32, tmp)
        part_b = sb("part_b", [P, IC], BF16, tmp)
        parts_of = ([0, 1, 2, 3], [2, 3, 0, 1, 4, 5, 6])
        moved = [sb(f"moved{o}", [P, len(parts_of[o]), NC], F32, tmp) for o in range(2)]
        hot = [sb(f"hot{o}", [P, U, RADIX + HIGH], BF16, tmp) for o in range(2)]
        base = [sb(f"base{o}", [P, RADIX + HIGH], F32, tmp) for o in range(2)]
        nought = sb("nought", [P, RADIX], F32, tmp)
        picked_row = sb("picked_row", [P, 2, RADIX], BF16, tmp)
        pos = [sb(f"pos{o}", [P, IC], F32, tmp) for o in range(2)]
        pos_i = [sb(f"pos_i{o}", [P, 3, IC], I32, tmp) for o in range(2)]
        row_of = [sb(f"row_of{o}", [P, IC], F32, tmp) for o in range(2)]
        col_of = [sb(f"col_of{o}", [P, IC], F32, tmp) for o in range(2)]
        wrap = sb("wrap", [P, 2, IC], F32, tmp)
        hot_row = [sb(f"hot_row{o}", [P, 2, P], BF16, tmp) for o in range(2)]
        hot_col = [sb(f"hot_col{o}", [P, 2, len(parts_of[o]), NC], BF16, tmp) for o in range(2)]
        slot_at = sb("slot_at", [P, NC], F32, tmp)
        key = [sb(f"key{o}", [P, NC + 2], F32, tmp) for o in range(2)]
        other = sb("other", [P, NC], F32, tmp)
        nxt = sb("nxt", [P, NC], F32, tmp)
        work = sb("work", [P, 2, NC], F32, tmp)
        stay = sb("stay", [P, P], F32, tmp)
        wrap_in = sb("wrap_in", [P, P], F32, tmp)
        up = sb("up", [P, P], F32, tmp)
        up_wrap = sb("up_wrap", [P, P], F32, tmp)
        down = sb("down", [P, P], F32, tmp)
        down_wrap = sb("down_wrap", [P, P], F32, tmp)
        indeg = sb("indeg", [IH, 2, RADIX], F32, tmp)
        deg = sb("deg", [IH, 2, RADIX], F32, tmp)
        dinv_n = sb("dinv_n", [IH, 2, RADIX], F32, tmp)
        newton = sb("newton", [IH, 2, RADIX], F32, tmp)
        zero_row = sb("zero_row", [P, XW * NPAD // (P * 49)], F32, tmp)

        consts = sem("consts")
        padded = sem("padded")
        edges_in = sem("edges_in")
        zeroed = sem("zeroed")
        setup_dve = sem("setup_dve")
        digits_up = sem("digits_up")
        hot_made = Count(sem("hot_made"), 1, IC)
        hot_counted = Count(sem("hot_counted"), 1, IC)
        base_in = Count(sem("base_in"), 1)
        ranked = Count(sem("ranked"), 2, IC)
        picked = Count(sem("picked"), 2, IC)
        folded = Count(sem("folded"), 1, IC)
        spread = Count(sem("spread"), 1, IC)
        placed = Count(sem("placed"), 1, IC)
        ready_pass = sem("ready_pass")
        ready_move = sem("ready_move")
        lnout = sem("lnout")
        turned = sem("turned")
        table_out = sem("table_out")
        diag_made = [Count(sem(f"diag_made{o}"), 1, NC // 4) for o in range(2)]
        keys_wide = [Count(sem(f"keys_wide{o}"), 1, NC // 4) for o in range(2)]
        same_made = [Count(sem(f"same_made{o}"), 1, NC // 4) for o in range(2)]

        def sort_sync(sp):
            sp.wait_ge(padded, 1)
            full = (E // P - IH)
            for a, (to, of) in enumerate(((raw[0], dst), (raw[1], src), (raw_w, edge_weight))):
                sp.dma_start(to[:, 0, :], of[0:IH * P].rearrange("(r k) -> r k", k=P)).then_inc(edges_in, 16)
                sp.dma_start(to[0:full, 1, :],
                             of[IH * P:(IH + full) * P].rearrange("(r k) -> r k", k=P)).then_inc(edges_in, 16)
                sp.dma_start(to[full:full + 1, 1, 0:E % P],
                             of[(IH + full) * P:E].rearrange("(r k) -> r k", r=1)).then_inc(edges_in, 16)
            flat = [t.rearrange("(i p r) d -> i p (r d)", i=49, p=P) for t in (sums, sums_gat, sums_src)]
            with sp.Fori(0, 49) as i:
                for t in flat:
                    w = t.shape[-1]
                    sp.dma_start(t[bass.ds(i, 1), :, :].rearrange("i p w -> p (i w)"),
                                 zero_row[:, 0:w]).then_inc(zeroed, 16)
            sp.wait_ge(lnout, 3)
            sp.dma_start(dinv_tab.rearrange("(h r l) o -> r h (l o)", h=2, l=RADIX),
                         dinv_n[:, :, :]).then_inc(table_out, 16)
            sp.wait_ge(table_out, 16)
            sp.wait_ge(zeroed, 16 * 49 * 3)

        def sort_pool(pool):
            for t in (ident, flip, stay, wrap_in, up, up_wrap, down, down_wrap):
                nc.gpsimd.memset(t[:, :], 0.0)
            nc.gpsimd.memset(before[:, :], 1.0)
            nc.gpsimd.memset(not0[:, :], 1.0)
            nc.gpsimd.memset(is0[:, :], 0.0).then_inc(consts, 1)
            nc.gpsimd.memset(neg0[:, :], 0.0).then_inc(consts, 1)
            pool.wait_ge(consts, 2)

            def put(t, base_v, cm, pat, op=ALU.not_equal, fill=1.0):
                return nc.gpsimd.affine_select(out=t, in_=t, pattern=pat, compare_op=op, fill=fill,
                                               base=base_v, channel_multiplier=cm)
            put(ident[:, :], 0, 1, [[-1, P]])
            put(flip[:, :], 1 - P, 1, [[1, P]])
            put(stay[:, 1:P], -1, 1, [[-1, P - 1]])
            put(wrap_in[:, 0:1], 1 - P, 1, [[0, 1]])
            put(up[:, :], -1, 1, [[-1, P]])
            put(up_wrap[:, P - 1:P], -1, 1, [[0, 1]])
            put(down[:, 2:P], -1, 1, [[-1, P - 2]])
            put(down_wrap[:, 1:2], 1 - P, 1, [[0, 1]])
            put(before[:, :], 0, -1, [[1, P]], ALU.is_gt, 0.0)
            put(not0[:, :], 0, 1, [[0, 1]], ALU.not_equal, 0.0)
            put(is0[:, :], 0, 1, [[0, 1]], ALU.not_equal, 1.0)
            put(neg0[:, :], 0, 1, [[0, 1]], ALU.not_equal, -BIG).then_inc(consts, 1)
            nc.gpsimd.iota(counting[:, :], [[1, RADIX]], base=0, channel_multiplier=0,
                           allow_small_or_imprecise_dtypes=True)
            nc.gpsimd.iota(slot_at[:, :], [[EC, NC]], base=-1, channel_multiplier=1,
                           allow_small_or_imprecise_dtypes=True).then_inc(consts, 1)

        def sort_dve(dve):
            v = nc.vector
            n_line = [0]

            def line(ins):
                n_line[0] += 1
                ins.then_inc(setup_dve, 1)
                dve.wait_ge(setup_dve, n_line[0])

            v.memset(zero_row[:, :], 0.0)
            v.memset(raw[0][:, :, :], PAD)
            v.memset(raw[1][:, :, :], PAD)
            v.memset(raw_w[:, :, :], 0.0).then_inc(padded, 1)
            v.memset(nought[:, :], 0.0)
            v.memset(ones_f[:, :], 1.0)
            v.memset(ones_b[:, :], 1.0)
            for o in range(2):
                v.memset(key[o][:, :], -1.0)
            dve.wait_ge(consts, 4)
            line(v.tensor_scalar(upto[:, :], before[:, :], -1.0, 1.0, ALU.mult, ALU.add))
            dve.wait_ge(edges_in, 16 * 9)
            for a in range(2):
                v.tensor_scalar(digit_i[:, 2 * a, :, :], raw[a][:, :, :], RADIX - 1, None, ALU.bitwise_and)
                line(v.tensor_scalar(digit_i[:, 2 * a + 1, :, :], raw[a][:, :, :], 8, None,
                                     ALU.logical_shift_right))
            line(v.tensor_copy(digit_f[:, :, :, :], digit_i[:, :, :, :]))
            dve.wait_ge(digits_up, 1)
            for b in range(2):
                v.tensor_copy(part[:, 2 * b:2 * b + 2, :],
                              bank[b][:, 0:2 * IC].rearrange("p (a c) -> p a c", a=2))
            line(v.tensor_copy(work[:, 0, 0:IC], bank[2][:, 0:IC]))
            for q in range(3):
                line(v.tensor_copy(part_b[:, :], work[:, q % 2, 0:IC]))
                line(v.tensor_copy(part[:, 4 + q, :], part_b[:, :]))
                if q < 2:
                    line(v.tensor_tensor(work[:, 1 - q % 2, 0:IC], work[:, q % 2, 0:IC],
                                         part[:, 4 + q, :], ALU.subtract))

            def one_hots(g, s, t):
                if started(g):
                    dve.wait_ge(hot_counted.sem, hot_counted.at(g - U))
                for o in range(2):
                    v.tensor_scalar(hot[o][:, s, 0:RADIX], counting[:, :],
                                    part[:, 2 * o, bass.ds(g, 1)], None, ALU.is_equal)
                    last = v.tensor_scalar(hot[o][:, s, RADIX:], counting[:, 0:HIGH],
                                           part[:, 2 * o + 1, bass.ds(g, 1)], None, ALU.is_equal)
                last.then_inc(hot_made.sem, 1)
            rounds(dve, IC, [(0, one_hots)])

            dve.wait_ge(hot_counted.sem, hot_counted.at(IC - 1))
            for o in range(2):
                for lo, hi in ((0, RADIX), (RADIX, RADIX + HIGH)):
                    line(v.tensor_tensor_scan(base[o][:, lo:hi], nought[:, 0:hi - lo], bank[o][:, lo:hi],
                                              0.0, ALU.add, ALU.add))
                line(v.tensor_tensor(base[o][:, :], base[o][:, :], bank[o][:, 0:RADIX + HIGH], ALU.subtract))
            for h in range(2):
                line(v.tensor_copy(indeg[:, h, :], bank[2 + h][0:IH, 0:RADIX]))
            v.tensor_scalar(deg[:, :, :], indeg[:, :, :], 1.0, None, ALU.add).then_inc(ready_pass, 1)

            def newton_step(dve):
                dve.wait_ge(lnout, 2)
                line(v.tensor_tensor(newton[:, :, :], dinv_n[:, :, :], dinv_n[:, :, :], ALU.mult))
                line(v.tensor_tensor(newton[:, :, :], newton[:, :, :], deg[:, :, :], ALU.mult))
                line(v.tensor_scalar(newton[:, :, :], newton[:, :, :], -0.5, 1.5, ALU.mult, ALU.add))
                v.tensor_tensor(dinv_n[:, :, :], dinv_n[:, :, :], newton[:, :, :], ALU.mult).then_inc(lnout, 1)

            for q in range(2):
                width = (RADIX, HIGH)[q]
                cols = (IC, NC)[q]

                def digit(o, g):
                    if q == 0:
                        return part[:, 2 * o, bass.ds(g, 1)]
                    return moved[o][:, 1, bass.ds(g, 1)]

                def hot_digit(g, s, t, q=q, width=width, digit=digit):
                    if started(g):
                        dve.wait_ge(folded.sem, folded.at(g - U, run=q))
                    for o in range(2):
                        last = v.tensor_scalar(hot[o][:, s, 0:width], counting[:, 0:width], digit(o, g),
                                               None, ALU.is_equal)
                    last.then_inc(hot_made.sem, 1)

                def pick(g, s, t, q=q, width=width):
                    for o in range(2):
                        dve.wait_ge(ranked.sem, ranked.at(g, o + 1, run=q))
                        v.scalar_tensor_tensor(picked_row[:, o, 0:width], bank[o][:, 0:width], 1.0,
                                               hot[o][:, s, 0:width], ALU.mult, ALU.mult,
                                               accum_out=pos[o][:, bass.ds(g, 1)]).then_inc(picked.sem, 1)
                rounds(dve, IC, [(0, hot_digit), (1, pick)])
                dve.wait_ge(picked.sem, picked.at(IC - 1, run=q))

                for o in range(2):
                    line(v.tensor_copy(pos_i[o][:, 0, :], pos[o][:, :]))
                    line(v.tensor_scalar(pos_i[o][:, 1, :], pos_i[o][:, 0, :], 7, None,
                                         ALU.logical_shift_right))
                    line(v.tensor_scalar(pos_i[o][:, 2, :], pos_i[o][:, 0, :], P - 1, None, ALU.bitwise_and))
                    line(v.tensor_copy(col_of[o][:, :], pos_i[o][:, 1, :]))
                    line(v.tensor_copy(row_of[o][:, :], pos_i[o][:, 2, :]))
                    if q == 1:
                        line(v.tensor_tensor(row_of[o][:, :], row_of[o][:, :], col_of[o][:, :], ALU.add))
                        v.tensor_scalar(wrap[:, 0, :], row_of[o][:, :], float(EC), None, ALU.is_ge)
                        line(v.tensor_scalar(wrap[:, 1, :], row_of[o][:, :], float(2 * EC), None, ALU.is_ge))
                        line(v.tensor_tensor(wrap[:, 0, :], wrap[:, 0, :], wrap[:, 1, :], ALU.add))
                        line(v.tensor_tensor(col_of[o][:, :], col_of[o][:, :], wrap[:, 0, :], ALU.add))
                        line(v.tensor_scalar(wrap[:, 0, :], wrap[:, 0, :], -float(EC), 1.0, ALU.mult, ALU.add))
                        line(v.tensor_tensor(row_of[o][:, :], row_of[o][:, :], wrap[:, 0, :], ALU.add))
                if q == 0:
                    newton_step(dve)

                def spread_out(g, s, t, q=q, cols=cols):
                    s = s % 2
                    if started(g, 2):
                        dve.wait_ge(placed.sem, placed.at(g - 2, run=q))
                    for o in range(2):
                        v.tensor_scalar(hot_row[o][:, s, :], counting[:, 0:P], row_of[o][:, bass.ds(g, 1)],
                                        None, ALU.is_equal)
                        for k, a in enumerate(parts_of[o]):
                            value = part[:, a, bass.ds(g, 1)] if q == 0 else moved[o][:, k, bass.ds(g, 1)]
                            last = v.tensor_scalar(hot_col[o][:, s, k, 0:cols], counting[:, 0:cols],
                                                   col_of[o][:, bass.ds(g, 1)], value,
                                                   ALU.is_equal, ALU.mult)
                    last.then_inc(spread.sem, 1)
                rounds(dve, IC, [(0, spread_out)])
                dve.wait_ge(placed.sem, placed.at(IC - 1, run=q))
                for o in range(2):
                    n = len(parts_of[o])
                    for k in range(0, n, 2):
                        m = min(2, n - k)
                        last = v.tensor_copy(moved[o][:, k:k + m, 0:cols],
                                             bank[2 + 2 * o + k // 2][:, 0:m * cols]
                                             .rearrange("p (a c) -> p a c", a=m))
                line(last)
                dve.sem_inc(ready_pass, 1)

            line(v.tensor_scalar(work[:, 0, :], slot_at[:, :], float(E) - 0.5, None, ALU.is_le))
            line(v.tensor_scalar(work[:, 1, :], work[:, 0, :], -float(PAD), float(PAD), ALU.mult, ALU.add))
            for o in range(2):
                k_main = key[o][:, 1:NC + 1]
                line(v.scalar_tensor_tensor(k_main, moved[o][:, 1, :], float(RADIX), moved[o][:, 0, :],
                                            ALU.mult, ALU.add))
                line(v.tensor_tensor(k_main, k_main, work[:, 0, :], ALU.mult))
                line(v.tensor_tensor(k_main, k_main, work[:, 1, :], ALU.add))
                line(v.scalar_tensor_tensor(other[:, :], moved[o][:, 3, :], float(RADIX), moved[o][:, 2, :],
                                            ALU.mult, ALU.add))
                line(v.tensor_tensor(other[:, :], other[:, :], work[:, 0, :], ALU.mult))
                line(v.tensor_copy(at[o][:, :, 0], other[:, :]))
            line(v.tensor_tensor(weight[:, :], moved[1][:, 6, :], moved[1][:, 5, :], ALU.add))
            line(v.tensor_tensor(weight[:, :], weight[:, :], moved[1][:, 4, :], ALU.add))
            line(v.tensor_scalar(weight[:, :], weight[:, :], not0[:, 0:1], is0[:, 0:1], ALU.mult, ALU.add))
            dve.sem_inc(ready_pass, 1)
            for o in range(2):
                dve.wait_ge(turned, 2 + o)
                v.tensor_copy(key_in[o][:, :], bank[0][:, 0:NC])
                line(v.tensor_copy(key_out[o][:, :], bank[1][:, 0:NC]))
                line(v.tensor_copy(nxt[:, :], bank[2][:, 0:NC]))
                line(v.tensor_tensor(work[:, 0, :], key_out[o][:, :], nxt[:, :], ALU.is_equal))
                line(v.tensor_scalar(work[:, 0, :], work[:, 0, :], is0[:, 0:1], float(FAR), ALU.max, ALU.mult))
                line(v.tensor_tensor(work[:, 0, :], work[:, 0, :], key_out[o][:, :], ALU.add))
                line(v.tensor_copy(at[o][:, :, 1], work[:, 0, :]))
                if o == 0:
                    line(v.tensor_tensor(gate_bwd[:, :], key_out[0][:, :], nxt[:, :], ALU.not_equal))
                    line(v.tensor_scalar(gate_bwd[:, :], gate_bwd[:, :], not0[:, 0:1], -BIG,
                                         ALU.mult, ALU.mult))
                    line(v.tensor_tensor(first[:, :], key[0][:, 1:NC + 1], bank[3][:, 0:NC], ALU.not_equal))
                    line(v.tensor_scalar(first[:, :], first[:, :], not0[:, 0:1], None, ALU.mult))
                    line(v.tensor_scalar(gate_fwd[:, :], first[:, :], -BIG, None, ALU.mult))
                    line(v.tensor_scalar(work[:, 0, :], key[0][:, 1:NC + 1], float(N) - 0.5, not0[:, 0:1],
                                         ALU.is_le, ALU.mult))
                    line(v.tensor_tensor(work[:, 0, :], work[:, 0, :], key[0][:, 1:NC + 1], ALU.mult))
                    line(v.tensor_copy(at[0][:, :, 2], work[:, 0, :]))
                dve.sem_inc(ready_pass, 1)

            dve.wait_ge(turned, 4)
            line(v.tensor_copy(dinv[:, :, :], bank[4][:, 0:NG * J].rearrange("p (j g) -> p g j", j=J)))
            line(v.tensor_tensor(dinv2[:, :, :], dinv[:, :, :], dinv[:, :, :], ALU.mult))
            indeg_t = bank[5][:, 0:NG * J].rearrange("p (j g) -> p g j", j=J)
            line(v.tensor_scalar(rdeg[:, :, :], indeg_t, 1.0, None, ALU.max))
            line(v.reciprocal(rdeg[:, :, :], rdeg[:, :, :]))
            line(v.tensor_scalar(has_in[:, :, :], indeg_t, 1.0, None, ALU.min))
            make_same(dve, 0)

        def make_same(dve, o):
            v = nc.vector

            def spread_keys(g, s, t):
                s = s % 2
                if started(g, 2):
                    dve.wait_ge(keys_wide[o].sem, keys_wide[o].at(g - 2))
                v.tensor_tensor(diag[:, s, :, :], ident[:, :].unsqueeze(1).to_broadcast([P, 4, P]),
                                key_out[o][:, bass.ds(g * 4, 4)].unsqueeze(2).to_broadcast([P, 4, P]),
                                ALU.mult).then_inc(diag_made[o].sem, 1)

            def compare(g, s, t):
                s = s % 2
                dve.wait_ge(keys_wide[o].sem, keys_wide[o].at(g))
                v.tensor_tensor(same[:, bass.ds(g * 4, 4), :],
                                bank[6 + s][:, :].rearrange("p (c m) -> p c m", c=4),
                                key_in[o][:, bass.ds(g * 4, 4)].unsqueeze(2).to_broadcast([P, 4, P]),
                                ALU.is_equal).then_inc(same_made[o].sem, 1)
            rounds(dve, NC // 4, [(0, spread_keys), (1, compare)], 2)

        def make_same_pe(pe, o):
            def widen(g, s, t):
                s = s % 2
                pe.wait_ge(diag_made[o].sem, diag_made[o].at(g))
                if started(g, 2):
                    pe.wait_ge(same_made[o].sem, same_made[o].at(g - 2))
                nc.tensor.matmul(bank[6 + s][:, :], ones_f[:, :],
                                 diag[:, s, :, :].rearrange("p c m -> p (c m)"),
                                 start=True, stop=True).then_inc(keys_wide[o].sem, 1)
            rounds(pe, NC // 4, [(0, widen)], 2)

        def sort_pe(pe):
            m = nc.tensor
            pe.wait_ge(consts, 4)
            pe.wait_ge(edges_in, 16 * 9)
            pe.wait_ge(setup_dve, 4)
            for a in range(5):
                for h in range(2):
                    of = digit_f[:, a, h, :] if a < 4 else raw_w[:, h, :]
                    at = (a % 2) * IC + h * IH
                    last = m.transpose(bank[a // 2][:, at:at + IH], of, ident[0:IH, 0:IH])
            last.then_inc(digits_up, 1)

            def histogram(g, s, t):
                first_one = isinstance(g, int) and g == 0
                pe.wait_ge(hot_made.sem, hot_made.at(g))
                kw = dict(start=first_one, stop=True, skip_group_check=True)
                for o in range(2):
                    m.matmul(bank[o][:, 0:RADIX + HIGH], ones_b[:, :], hot[o][:, s, :], **kw)
                for h in range(2):
                    last = m.matmul(bank[2 + h][0:IH, 0:RADIX],
                                    hot[0][:, s, RADIX + h * IH:RADIX + (h + 1) * IH],
                                    hot[0][:, s, 0:RADIX], **kw)
                last.then_inc(hot_counted.sem, 1)
            pe.wait_ge(setup_dve, 4 + 1 + 8)
            rounds(pe, IC, [(0, histogram)])

            for q in range(2):
                width = (RADIX, HIGH)[q]
                cols = (IC, NC)[q]
                pe.wait_ge(ready_pass, 1 + q)
                for o in range(2):
                    m.matmul(bank[o][:, 0:width], ident[:, :],
                             base[o][:, q * RADIX:q * RADIX + width], start=True, stop=True,
                             skip_group_check=True)

                def rank(g, s, t, q=q, width=width):
                    pe.wait_ge(hot_made.sem, hot_made.at(g, run=q + 1))
                    kw = dict(start=False, stop=True, skip_group_check=True)
                    for o in range(2):
                        m.matmul(bank[o][:, 0:width], before[:, :], hot[o][:, s, 0:width],
                                 **kw).then_inc(ranked.sem, 1)
                    for o in range(2):
                        pe.wait_ge(picked.sem, picked.at(g, o + 1, run=q))
                        last = m.matmul(bank[o][:, 0:width], upto[:, :], hot[o][:, s, 0:width], **kw)
                    last.then_inc(folded.sem, 1)
                rounds(pe, IC, [(0, rank)])

                def place(g, s, t, q=q, cols=cols):
                    s = s % 2
                    first_one = isinstance(g, int) and g == 0
                    pe.wait_ge(spread.sem, spread.at(g, run=q))
                    for o in range(2):
                        n = len(parts_of[o])
                        for k in range(0, n, 2):
                            w = min(2, n - k)
                            last = m.matmul(bank[2 + 2 * o + k // 2][:, 0:w * cols]
                                            .rearrange("p (a c) -> p a c", a=w),
                                            hot_row[o][:, s, :], hot_col[o][:, s, k:k + w, 0:cols],
                                            start=first_one, stop=True, skip_group_check=True)
                    last.then_inc(placed.sem, 1)
                rounds(pe, IC, [(0, place)])

            pe.wait_ge(ready_pass, 4)
            for o in range(2):
                if o:
                    pe.wait_ge(ready_pass, 5)
                k = key[o]
                for b, pairs in enumerate((((stay, 1), (wrap_in, 0)), ((stay, 1), (wrap_in, 1)),
                                           ((up, 1), (up_wrap, 2)), ((down, 1), (down_wrap, 0)))):
                    for n, (shift, at) in enumerate(pairs):
                        last = m.matmul(bank[b][:, 0:NC], shift[:, :], k[:, at:at + NC],
                                        start=n == 0, stop=n == 1)
                if o == 0:
                    m_first = last
                last.then_inc(turned, 1 if o else 2)
            pe.wait_ge(lnout, 3)
            for b, t in ((4, dinv_n), (5, indeg)):
                for j in range(J):
                    for h in range(2):
                        last = m.transpose(bank[b][:, j * NG + h * IH:j * NG + (h + 1) * IH],
                                           t[:, h, j:RADIX:J], ident[0:IH, 0:IH])
            last.then_inc(turned, 1)
            make_same_pe(pe, 0)

        def sort_act(act):
            act.wait_ge(ready_pass, 1)
            nc.scalar.activation(dinv_n[:, :, :], deg[:, :, :], ACT.Ln).then_inc(lnout, 1)
            act.wait_ge(lnout, 1)
            nc.scalar.activation(dinv_n[:, :, :], dinv_n[:, :, :], ACT.Exp, scale=-0.5).then_inc(lnout, 1)

        w0_in = sb("w0_in", [P, 2, D], F32, tmp)
        att_row = sb("att_row", [P, 2, D], F32, tmp)
        att_mul = sb("att_mul", [P, 2, D], F32, tmp)
        g_col = sb("g_col", [P, 2], F32, tmp)
        b_col = sb("b_col", [P, 2], F32, tmp)
        w_m1_in = sb("w_m1_in", [P, 2, D], F32, tmp)
        weights_in = sem("weights_in")
        weights_dve = sem("weights_dve")
        weights_pe = sem("weights_pe")
        N_WEIGHTS = 17

        def weights_sync(sp):
            def load(to, of):
                sp.dma_start(to, of).then_inc(weights_in, 16)
            for to, of in ((w0_in, W0), (w_self, Wself), (w_neigh, Wneigh), (w_gat, Wg),
                           (w_m1_in, Wm1), (w_m2, Wm2), (w_l3, Wl3)):
                load(to[:, :, :], of.rearrange("(t p) n -> p t n", p=P))
            for to, of in zip(rows.values(), (b0, b1, gat_bias, bm2, bl3)):
                load(to[:, :], of.rearrange("(o d) -> o d", o=1).to_broadcast([P, D]))
            for k, of in enumerate((att_src, att_dst)):
                load(att_row[:, k, :], of.rearrange("(o h) d -> o (h d)", o=1).to_broadcast([P, D]))
            with nc.allow_non_contiguous_dma(reason="three vectors of 256, feature by partition"):
                for to, of in ((g_col, ln_g), (b_col, ln_b), (m1_col, bm1)):
                    load(to[:, :], of.rearrange("(t p) -> p t", p=P))

        def weights_vec(dve):
            v = nc.vector
            dve.wait_ge(weights_in, 16 * N_WEIGHTS)
            n_line = [0]

            def line(ins):
                n_line[0] += 1
                ins.then_inc(weights_dve, 1)
                dve.wait_ge(weights_dve, n_line[0])
            v.memset(eps[:, :], 1e-5)
            for k in range(2):
                line(v.tensor_tensor(att_mul[:, :, :], w_gat[:, :, :],
                                     att_row[:, k, :].unsqueeze(1).to_broadcast([P, 2, D]), ALU.mult))
                line(v.tensor_reduce(w_att[:, :, k * HEADS:(k + 1) * HEADS],
                                     att_mul[:, :, :].rearrange("p t (h d) -> p t h d", d=HD), AXX, ALU.add))
            for t in range(2):
                line(v.tensor_scalar(w_m1[:, t, :], w_m1_in[:, t, :], g_col[:, t:t + 1], None, ALU.mult))
            dve.wait_ge(weights_pe, 1)
            for t in range(2):
                line(v.tensor_copy(w0t[:, t, :], bank[t][:, 0:D]))
            line(v.tensor_tensor(m1_col[:, :], m1_col[:, :], bank[2][:, 0:2], ALU.add))

        def weights_tensor(pe):
            m = nc.tensor
            pe.wait_ge(weights_in, 16 * N_WEIGHTS)
            pe.wait_ge(same_made[0].sem, same_made[0].at(NC // 4 - 1))
            for kt in range(2):
                for nt in range(2):
                    m.transpose(bank[kt][:, nt * P:(nt + 1) * P], w0_in[:, nt, kt * P:(kt + 1) * P], ident[:, :])
            for f in range(2):
                for t in range(2):
                    last = m.matmul(bank[2][:, f:f + 1], w_m1_in[:, t, f * P:(f + 1) * P], b_col[:, t:t + 1],
                                    start=t == 0, stop=t == 1)
            last.then_inc(weights_pe, 1)

        tmp.close()

        got = sb("got", [P, U, XW])
        done = sb("done", [P, U, XW])
        near = sb("near", [P, U, P])
        from_at = sb("from_at", [P, U, 2], I32)
        to_at = sb("to_at", [P, U], I32)
        d_got = sb("d_got", [P, U, 1])
        d_edge = sb("d_edge", [P, U, 1])
        RUNS = 5
        tables_done = sem("tables_done")
        from_made = Count(sem("from_made"), 1, NC)
        to_made = Count(sem("to_made"), 1, NC)
        near_made = Count(sem("near_made"), 1, NC)
        d_ready = Count(sem("d_ready"), 1, NC)
        scaled = Count(sem("scaled"), 1, NC)
        carried = Count(sem("carried"), 1, NC)
        summed = Count(sem("summed"), 1, NC)
        copied = Count(sem("copied"), 1, NC)
        gathered = [sem(f"gathered{s}") for s in range(U)]
        d_gathered = [sem(f"d_gathered{s}") for s in range(U)]
        scattered = [sem(f"scattered{s}") for s in range(U)]
        held = sem("held")

        order_of = (0, 0, 0, 0, 1)
        width_of = (D, D, D, XW, D)
        from_of = (x, y1, x1, xp, x3)
        to_of = (sums, sums, sums, sums_gat, sums_src)

        def landed(run, t):
            return 16 * (run * (NC // U) + 1) + t * 16

        def edges_pool(pool, run):
            o, w = order_of[run], width_of[run]

            def gather(c, s, t):
                pool.wait_ge(from_made.sem, from_made.at(c, run=run))
                if started(c):
                    pool.wait_ge(summed.sem, summed.at(c - U, run=run))
                pool.sem_inc(held, 1)
                nc.gpsimd.indirect_dma_start(
                    got[:, s, 0:D], None, from_of[run],
                    bass.IndirectOffsetOnAxis(ap=from_at[:, s, 0:1], axis=0),
                    bounds_check=N - 1, oob_is_err=False).then_inc(gathered[s], 16)
                if run == 0:
                    nc.gpsimd.indirect_dma_start(
                        d_got[:, s, :], None, dinv_tab,
                        bass.IndirectOffsetOnAxis(ap=from_at[:, s, 0:1], axis=0),
                        bounds_check=N - 1, oob_is_err=False).then_inc(d_gathered[s], 16)

            def scatter(c, s, t):
                pool.wait_ge(to_made.sem, to_made.at(c, run=run))
                pool.wait_ge(copied.sem, copied.at(c, run=run))
                pool.sem_inc(held, 1)
                nc.gpsimd.indirect_dma_start(
                    to_of[run], bass.IndirectOffsetOnAxis(ap=to_at[:, s:s + 1], axis=0),
                    done[:, s, 0:w], None, bounds_check=N - 1, oob_is_err=False).then_inc(scattered[s], 16)

            pool.wait_ge(tables_done, run + 1)
            rounds(pool, NC, [(0, gather), (4, scatter)])

        def edges_dve(dve, run):
            v = nc.vector
            o, w = order_of[run], width_of[run]

            def columns(c, s, t):
                if started(c) or run:
                    dve.wait_ge(gathered[s], landed(run, t) - 16)
                    if run == 0:
                        dve.wait_ge(d_gathered[s], landed(run, t) - 16)
                dve.sem_inc(held, 1)
                v.tensor_copy(from_at[:, s, 0:1], at[o][:, bass.ds(c, 1), 0]).then_inc(from_made.sem, 1)

            def weigh(c, s, t):
                if run == 0:
                    dve.wait_ge(d_gathered[s], landed(run, t))
                    v.tensor_scalar(d_edge[:, s, :], d_got[:, s, :], not0[:, 0:1], is0[:, 0:1],
                                    ALU.mult, ALU.add).then_inc(d_ready.sem, 1)
                    dve.wait_ge(d_ready.sem, d_ready.at(c))
                if started(c):
                    dve.wait_ge(summed.sem, summed.at(c - U, run=run))
                by = (d_edge[:, s, :] if run == 0 else weight[:, bass.ds(c, 1)] if run == 4 else 1.0)
                v.tensor_scalar(near[:, s, :], same[:, bass.ds(c, 1), :].rearrange("p c m -> p (c m)"),
                                by, None, ALU.mult).then_inc(near_made.sem, 1)
                if run == 3:
                    dve.wait_ge(gathered[s], landed(run, t))
                    v.tensor_tensor(got[:, s, 0:D].rearrange("p (h d) -> p h d", d=HD),
                                    got[:, s, 0:D].rearrange("p (h d) -> p h d", d=HD),
                                    p_and_m[:, bass.ds(c, 1), 0:HEADS].rearrange("p c h -> p (c h)")
                                    .unsqueeze(2).to_broadcast([P, HEADS, HD]), ALU.mult)
                    v.tensor_scalar(got[:, s, D:XW], p_and_m[:, bass.ds(c, 1), :].rearrange("p c h -> p (c h)"),
                                    1.0, None, ALU.mult).then_inc(scaled.sem, 1)

            def targets(c, s, t):
                if started(c) or run:
                    dve.wait_ge(scattered[s], landed(run, t) - 16)
                dve.sem_inc(held, 1)
                v.tensor_copy(to_at[:, s:s + 1], at[o][:, bass.ds(c, 1), 1]).then_inc(to_made.sem, 1)

            rounds(dve, NC, [(0, columns), (2, weigh), (3, targets)])

        def edges_pe(pe, run):
            w = width_of[run]

            def add(c, s, t):
                pe.wait_ge(near_made.sem, near_made.at(c, run=run))
                pe.wait_ge(carried.sem, carried.at(c, run=run))
                if started(c, 2):
                    pe.wait_ge(copied.sem, copied.at(c - 2, run=run))
                nc.tensor.matmul(bank[s % 2][:, 0:w], near[:, s, :], got[:, s, 0:w],
                                 start=True, stop=True).then_inc(summed.sem, 1)
            rounds(pe, NC, [(2, add)])

        def edges_act(act, run):
            w = width_of[run]

            def carry(c, s, t):
                if run == 3:
                    act.wait_ge(scaled.sem, scaled.at(c))
                act.wait_ge(gathered[s], landed(run, t))
                if isinstance(c, int) and c == 0:
                    nc.scalar.activation(got[0:1, s, 0:w], zero_w[0:1, 0:w], ACT.Copy).then_inc(carried.sem, 1)
                    return
                act.wait_ge(summed.sem, summed.at(c - 1, run=run))
                nc.scalar.activation(got[0:1, s, 0:w], bank[(s - 1) % 2][0:1, 0:w],
                                     ACT.Copy).then_inc(carried.sem, 1)

            def collect(c, s, t):
                act.wait_ge(summed.sem, summed.at(c, run=run))
                if started(c) or run:
                    act.wait_ge(scattered[s], landed(run, t) - 16)
                nc.scalar.activation(done[:, s, 0:w], bank[s % 2][:, 0:w], ACT.Copy).then_inc(copied.sem, 1)
            rounds(act, NC, [(2, carry), (3, collect)])

        zero_w_made = sem("zero_w_made")

        ends = sb("ends", [P, NC, 3 * HEADS])
        p_and_m = sb("p_and_m", [P, NC, 2 * HEADS])
        a_got = sb("a_got", [P, U, 2, 2 * HEADS])
        a_from = sb("a_from", [P, U, 2], I32)
        a_gathered = [sem(f"a_gathered{s}") for s in range(U)]
        a_from_made = Count(sem("a_from_made"), 1, NC)
        a_kept = Count(sem("a_kept"), 1, NC)
        piece = sb("piece", [P, 2, 2, 4, HEADS])
        turn = sb("turn", [P, 2, 4 * HEADS])
        NQ = NC // 4
        piece_made = Count(sem("piece_made"), 1, NQ)
        heads_up = Count(sem("heads_up"), 1, NQ)
        gates_in = Count(sem("gates_in"), 1, NQ)
        scanned = Count(sem("scanned"), 1, NQ)
        edges_up = Count(sem("edges_up"), 1, NQ)
        turned_in = Count(sem("turned_in"), 1, NQ)
        mirrored = Count(sem("mirrored"), 1, NQ)
        max_kept = Count(sem("max_kept"), 1, NQ)
        soft_dve = sem("soft_dve")
        soft_act = sem("soft_act")

        def attention_pool(pool):
            def gather(c, s, t):
                pool.wait_ge(a_from_made.sem, a_from_made.at(c))
                if started(c):
                    pool.wait_ge(a_kept.sem, a_kept.at(c - U))
                pool.sem_inc(held, 1)
                for k in range(2):
                    nc.gpsimd.indirect_dma_start(
                        a_got[:, s, k, :], None, a16,
                        bass.IndirectOffsetOnAxis(ap=a_from[:, s, k:k + 1], axis=0),
                        bounds_check=N - 1, oob_is_err=False).then_inc(a_gathered[s], 16)
            pool.wait_ge(tables_done, 4)
            rounds(pool, NC, [(0, gather)])

        def attention_dve(dve):
            v = nc.vector

            def columns(c, s, t):
                if started(c):
                    dve.wait_ge(a_gathered[s], 32 * t)
                dve.sem_inc(held, 1)
                v.tensor_copy(a_from[:, s, :], at[0][:, bass.ds(c, 1), 0:3:2].rearrange("p c k -> p (c k)")
                              ).then_inc(a_from_made.sem, 1)

            def keep(c, s, t):
                dve.wait_ge(a_gathered[s], 32 * t + 32)
                v.tensor_scalar(ends[:, bass.ds(c, 1), 0:HEADS].rearrange("p c h -> p (c h)"),
                                a_got[:, s, 0, 0:HEADS], not0[:, 0:1], neg0[:, 0:1], ALU.mult, ALU.add)
                v.tensor_scalar(ends[:, bass.ds(c, 1), HEADS:].rearrange("p c h -> p (c h)"),
                                a_got[:, s, 1, :], 1.0, None, ALU.mult).then_inc(a_kept.sem, 1)
            rounds(dve, NC, [(0, columns), (2, keep)])
            dve.wait_ge(a_kept.sem, a_kept.at(NC - 1))

            for back in range(2):
                source = run_max if back else ends
                gate = gate_bwd if back else gate_fwd

                def chunk(q, back=back):
                    return (NC - 4 - q * 4) if back else q * 4

                def lay(q, s, t, back=back, source=source, gate=gate, chunk=chunk):
                    if started(q, 2):
                        dve.wait_ge(heads_up.sem, heads_up.at(q - 2, run=back))
                    v.tensor_scalar(piece[:, s, 0, :, :], source[:, bass.ds(chunk(q), 4), 0:HEADS],
                                    1.0, None, ALU.mult)
                    v.tensor_scalar(piece[:, s, 1, :, :], gate[:, bass.ds(chunk(q), 4)].unsqueeze(2)
                                    .to_broadcast([P, 4, HEADS]), 1.0, None, ALU.mult
                                    ).then_inc(piece_made.sem, 1)

                def climb(q, s, t, back=back):
                    dve.wait_ge(gates_in.sem, gates_in.at(q, run=back))
                    if started(q, 1):
                        dve.wait_ge(scanned.sem, scanned.at(q - 1, run=back))
                    if started(q, 2):
                        dve.wait_ge(edges_up.sem, edges_up.at(q - 2, run=back))
                    start = -BIG if isinstance(q, int) and q == 0 else scan[:, 1 - s, 4 * P - 1:4 * P]
                    v.tensor_tensor_scan(scan[:, s, :], gates[:, s, :], bank[2 + s][0:HEADS, :], start,
                                         ALU.add, ALU.max).then_inc(scanned.sem, 1)

                def keep_max(q, s, t, back=back, chunk=chunk):
                    if back:
                        dve.wait_ge(mirrored.sem, mirrored.at(q))
                        v.tensor_scalar(p_and_m[:, bass.ds(chunk(q), 4), HEADS:],
                                        bank[6 + s][:, 64:96].rearrange("p (c h) -> p c h", h=HEADS),
                                        1.0, None, ALU.mult).then_inc(max_kept.sem, 1)
                    else:
                        dve.wait_ge(edges_up.sem, edges_up.at(q))
                        v.tensor_scalar(run_max[:, bass.ds(chunk(q), 4), :],
                                        bank[6 + s][:, 0:32].rearrange("p (c h) -> p c h", h=HEADS),
                                        not0[:, 0:1], neg0[:, 0:1], ALU.mult, ALU.add).then_inc(max_kept.sem, 1)
                rounds(dve, NQ, [(0, lay), (1, climb), (2, keep_max)], 2)
                dve.wait_ge(max_kept.sem, max_kept.at(NQ - 1, run=back))

            n_line = [0]

            def line(ins):
                n_line[0] += 1
                ins.then_inc(soft_dve, 1)
                dve.wait_ge(soft_dve, n_line[0])
            own, self_s, self_d = (ends[:, :, k * HEADS:(k + 1) * HEADS] for k in range(3))
            weights, top = p_and_m[:, :, 0:HEADS], p_and_m[:, :, HEADS:]
            line(v.tensor_tensor(top, top, self_s, ALU.max))
            line(v.tensor_tensor(top, top, self_d, ALU.add))
            line(v.scalar_tensor_tensor(top, top, 0.2, top, ALU.mult, ALU.max))
            line(v.tensor_tensor(own, own, self_d, ALU.add))
            line(v.scalar_tensor_tensor(own, own, 0.2, own, ALU.mult, ALU.max))
            line(v.tensor_tensor(weights, own, top, ALU.subtract))
            line(v.tensor_tensor(top, top, first[:, :].unsqueeze(2).to_broadcast([P, NC, HEADS]), ALU.mult))
            dve.wait_ge(soft_act, 1)

        def attention_pe(pe):
            m = nc.tensor
            for back in range(2):
                by = flip if back else ident

                def up_(q, s, t, back=back, by=by):
                    pe.wait_ge(piece_made.sem, piece_made.at(q, run=back))
                    if started(q, 2):
                        pe.wait_ge(scanned.sem, scanned.at(q - 2, run=back))
                        pe.wait_ge(gates_in.sem, gates_in.at(q - 2, run=back))
                    for k, b in ((0, 2), (1, 4)):
                        for c in range(4):
                            last = m.matmul(bank[b + s][0:HEADS, c * P:(c + 1) * P],
                                            piece[:, s, k, 3 - c if back else c, :], by[:, :],
                                            start=True, stop=True)
                    last.then_inc(heads_up.sem, 1)

                def down_(q, s, t, back=back):
                    pe.wait_ge(scanned.sem, scanned.at(q, run=back))
                    if started(q, 2):
                        pe.wait_ge(max_kept.sem, max_kept.at(q - 2, run=back))
                    for c in range(4):
                        at_c = (3 - c if back else c) * HEADS
                        last = m.matmul(bank[6 + s][:, at_c:at_c + HEADS], scan[:, s, c * P:(c + 1) * P],
                                        ident[0:HEADS, 0:HEADS], start=True, stop=True)
                    last.then_inc(edges_up.sem, 1)

                def mirror(q, s, t):
                    pe.wait_ge(turned_in.sem, turned_in.at(q))
                    m.matmul(bank[6 + s][:, 64:96], flip[:, :], turn[:, s, :],
                             start=True, stop=True).then_inc(mirrored.sem, 1)
                rounds(pe, NQ, [(0, up_), (1, down_)] + ([(2, mirror)] if back else []), 2)

        def attention_act(act):
            for back in range(2):
                def gates_copy(q, s, t, back=back):
                    act.wait_ge(heads_up.sem, heads_up.at(q, run=back))
                    if started(q, 2):
                        act.wait_ge(scanned.sem, scanned.at(q - 2, run=back))
                    nc.scalar.activation(gates[:, s, :], bank[4 + s][0:HEADS, :],
                                         ACT.Copy).then_inc(gates_in.sem, 1)

                def turn_copy(q, s, t):
                    act.wait_ge(edges_up.sem, edges_up.at(q, run=1))
                    if started(q, 2):
                        act.wait_ge(mirrored.sem, mirrored.at(q - 2))
                    nc.scalar.activation(turn[:, s, :], bank[6 + s][:, 0:32], ACT.Copy
                                         ).then_inc(turned_in.sem, 1)
                rounds(act, NQ, [(0, gates_copy)] + ([(1, turn_copy)] if back else []), 2)
            act.wait_ge(soft_dve, 6)
            weights = p_and_m[:, :, 0:HEADS]
            nc.scalar.activation(weights, weights, ACT.Exp).then_inc(soft_act, 1)

        RA = 2 * U
        ring_a = sb("ring_a", [P, RA, J, D])
        ring_s = sb("ring_s", [P, U, J, XW])
        ring_b = sb("ring_b", [P, U, J, D])
        ring_o = sb("ring_o", [P, U, J, D])
        ring_z = sb("ring_z", [P, 2, J, D])
        mix = sb("mix", [P, 2, J, D])
        feat = [sb(f"feat{k}", [P, 2, 2, J * P]) for k in range(2)]
        hid = sb("hid", [P, 2, 2, J * P])
        run_max = ring_a[:, :, :, :].rearrange("p s j d -> p (s j d)")[:, 0:NC * HEADS] \
            .rearrange("p (c h) -> p c h", h=HEADS)
        gates = ring_z[0:HEADS, :, :, :].rearrange("p s j d -> p s (j d)")
        scan = mix[0:HEADS, :, :, :].rearrange("p s j d -> p s (j d)")
        junk = sb("junk", [P, J, D], BF16)
        scores = sb("scores", [P, U, J, 2 * HEADS])
        small = sb("small", [P, U, 6, J * HEADS])
        stat = sb("stat", [P, 2, U, J, 6])
        mv = sb("mv", [P, 2, U, J, 2])
        norm = sb("norm", [P, 2, 4, U, J])
        soft = sb("soft", [P, 3, U, J])

        STEPS = 5
        loads_of = (2, 3, 2, 4, 2)
        stores_of = (1, 1, 3, 1, 1)
        loaded = [sem(f"loaded{s}") for s in range(U)]
        stored = [sem(f"stored{s}") for s in range(U)]
        NT = NG // U

        def loads(step, t):
            return 16 * sum(loads_of[:step]) * NT + 16 * loads_of[step] * (t + 1)

        def stores(step, t):
            return 16 * sum(stores_of[:step]) * NT + 16 * stores_of[step] * (t + 1)

        def group(table, g):
            return table[bass.ds(g * GROUP, GROUP), :].rearrange("(p j) d -> p j d", j=J)

        def flat(ap):
            return ap.rearrange("p j d -> p (j d)")

        def fetch(sp, table, g, buf, slot, ring_slot, w=D):
            if table is x and isinstance(g, int) and g == NG - 1:
                sp.dma_start(buf[0:LAST, slot, :, 0:w],
                             table[g * GROUP:N, :].rearrange("(p j) d -> p j d", j=J)
                             ).then_inc(loaded[ring_slot], 16)
            else:
                sp.dma_start(buf[:, slot, :, 0:w], group(table, g)).then_inc(loaded[ring_slot], 16)

        def put_out(sp, table, g, buf, slot):
            if table is out and isinstance(g, int) and g == NG - 1:
                sp.dma_start(table[g * GROUP:N, :].rearrange("(p j) d -> p j d", j=J),
                             buf[0:LAST, slot, :, :]).then_inc(stored[slot], 16)
            else:
                sp.dma_start(group(table, g), buf[:, slot, :, :]).then_inc(stored[slot], 16)

        def sums_complete(sp, step):
            for s in range(U):
                sp.wait_ge(scattered[s], landed(step, NC // U - 1))

        def step_complete(sp, step):
            for s in range(U):
                sp.wait_ge(stored[s], stores(step, NT - 1))
            sp.sem_inc(tables_done, 1)

        def norm_counts(name, k=0):
            return Count(sem(name + "_stats"), 3), Count(sem(name + "_roots"), 2), Count(sem(name + "_fixed"), 4), k

        def norm_stats(dve, counts, g, s, z):
            v = nc.vector
            stats, roots, fixed, k = counts
            for j in range(J):
                last = v.bn_stats(stat[:, k, s, j, :], z[:, j, :])
            last.then_inc(stats.sem, 1)
            dve.wait_ge(stats.sem, stats.at(g, 1))
            dve.sem_inc(held, 1)
            for j in range(J):
                last = v.bn_aggr(mv[:, k, s, j, :], stat[:, k, s, j, :])
            last.then_inc(stats.sem, 1)
            dve.wait_ge(stats.sem, stats.at(g, 2))
            v.tensor_scalar(norm[:, k, 0, s, :], mv[:, k, s, :, 1], 1e-5, None, ALU.add
                            ).then_inc(stats.sem, 1)

        def norm_roots(act, counts, g, s):
            stats, roots, fixed, k = counts
            act.wait_ge(stats.sem, stats.at(g))
            nc.scalar.activation(norm[:, k, 1, s, :], norm[:, k, 0, s, :], ACT.Ln).then_inc(roots.sem, 1)
            act.wait_ge(roots.sem, roots.at(g, 1))
            nc.scalar.activation(norm[:, k, 1, s, :], norm[:, k, 1, s, :], ACT.Exp,
                                 scale=-0.5).then_inc(roots.sem, 1)

        def norm_refine(dve, counts, g, s):
            v = nc.vector
            stats, roots, fixed, k = counts
            var, y, w, off = (norm[:, k, q, s, :] for q in range(4))
            dve.wait_ge(roots.sem, roots.at(g))
            v.scalar_tensor_tensor(w, y, -0.5, y, ALU.mult, ALU.mult).then_inc(fixed.sem, 1)
            dve.wait_ge(fixed.sem, fixed.at(g, 1))
            v.tensor_tensor(w, w, var, ALU.mult).then_inc(fixed.sem, 1)
            dve.wait_ge(fixed.sem, fixed.at(g, 2))
            v.scalar_tensor_tensor(y, w, 1.5, y, ALU.add, ALU.mult).then_inc(fixed.sem, 1)
            dve.wait_ge(fixed.sem, fixed.at(g, 3))
            v.scalar_tensor_tensor(off, mv[:, k, s, :, 0], -1.0, y, ALU.mult, ALU.mult
                                   ).then_inc(fixed.sem, 1)

        def norm_apply(act, counts, g, s, to, z, signal):
            stats, roots, fixed, k = counts
            act.wait_ge(fixed.sem, fixed.at(g))
            for j in range(J):
                last = nc.scalar.activation(to[:, j, :], z[:, j, :], ACT.Identity,
                                            bias=norm[:, k, 3, s, j:j + 1], scale=norm[:, k, 1, s, j:j + 1])
            last.then_inc(signal.sem, 1)

        def turn_rows(of, to):
            for h in range(2):
                for j in range(J):
                    last = nc.tensor.transpose(to[:, (h * J + j) * P:(h * J + j + 1) * P],
                                               of[:, j, h * P:(h + 1) * P], ident[:, :])
            return last

        def times(to, terms, w=D, at_=0):
            for j in range(J):
                n = 0
                for f, wt in terms:
                    for h in range(2):
                        last = nc.tensor.matmul(to[:, at_ + j * w:at_ + (j + 1) * w], f[:, h, j * P:(j + 1) * P],
                                                wt[:, h, :], start=n == 0, stop=n == 2 * len(terms) - 1)
                        n += 1
            return last

        def row2(r):
            return r[:, :].unsqueeze(1).to_broadcast([P, J, D])

        def psum2(b):
            return bank[b][:, :].rearrange("p (j d) -> p j d", j=J)

        a_sum = Count(sem("a_sum"))
        a_out = Count(sem("a_out"))

        def hop_sync(sp):
            def load(g, s, t):
                if started(g):
                    sp.wait_ge(a_sum.sem, a_sum.at(g - U))
                    sp.sem_inc(held, 1)
                fetch(sp, x, g, ring_a, s, s)
                fetch(sp, sums, g, ring_s, s, s)

            def store(g, s, t):
                sp.wait_ge(a_out.sem, a_out.at(g))
                sp.sem_inc(held, 1)
                put_out(sp, y1, g, ring_o, s)

            sums_complete(sp, 0)
            rounds(sp, NG, [(0, load), (2, store)], U, peel=True)
            step_complete(sp, 0)

        def hop_dve(dve):
            def add(g, s, t):
                dve.wait_ge(loaded[s], loads(0, t))
                if started(g, 2):
                    dve.wait_ge(a_out.sem, a_out.at(g - 2))
                for j in range(J):
                    last = nc.vector.scalar_tensor_tensor(
                        ring_z[:, s % 2, j, :], ring_a[:, s, j, :],
                        dinv[:, bass.ds(g, 1), j], ring_s[:, s, j, 0:D], ALU.mult, ALU.add)
                last.then_inc(a_sum.sem, 1)
            rounds(dve, NG, [(0, add)])

        def hop_act(act):
            def scale(g, s, t):
                act.wait_ge(a_sum.sem, a_sum.at(g))
                if started(g):
                    act.wait_ge(stored[s], stores(0, t - 1))
                act.sem_inc(held, 1)
                for j in range(J):
                    last = nc.scalar.activation(ring_o[:, s, j, :], ring_z[:, s % 2, j, :], ACT.Copy,
                                                scale=dinv2[:, bass.ds(g, 1), j])
                last.then_inc(a_out.sem, 1)
            rounds(act, NG, [(0, scale)])

        b_sum = Count(sem("b_sum"))
        b_up = Count(sem("b_up"))
        b_feat = Count(sem("b_feat"))
        b_logit = Count(sem("b_logit"))
        b_max = Count(sem("b_max"), 2)
        b_exp = Count(sem("b_exp"), 2)
        b_res = Count(sem("b_res"), 2)
        b_out = Count(sem("b_out"))
        b_norm = norm_counts("b_norm")
        logit = ring_b

        def sgc_sync(sp):
            def load(g, s, t):
                if started(g):
                    sp.wait_ge(b_sum.sem, b_sum.at(g - U))
                    sp.sem_inc(held, 1)
                fetch(sp, y1, g, ring_a, s, s)
                fetch(sp, sums, g, ring_s, s, s)

            def load_x(g, s, t):
                if started(g):
                    sp.wait_ge(b_res.sem, b_res.at(g - U))
                    sp.sem_inc(held, 1)
                fetch(sp, x, g, ring_a, U + s, s)

            def store(g, s, t):
                sp.wait_ge(b_out.sem, b_out.at(g))
                sp.sem_inc(held, 1)
                put_out(sp, x1, g, ring_o, s)

            sums_complete(sp, 1)
            rounds(sp, NG, [(0, load), (1, load_x), (4, store)], U, peel=True)
            step_complete(sp, 1)

        def sgc_dve(dve):
            v = nc.vector

            def add(g, s, t):
                dve.wait_ge(loaded[s], loads(1, t))
                if started(g, 2):
                    dve.wait_ge(b_up.sem, b_up.at(g - 2))
                v.tensor_tensor(mix[:, s % 2, :, :], ring_a[:, s, :, :], ring_s[:, s, :, 0:D], ALU.add
                                ).then_inc(b_sum.sem, 1)

            def bias(g, s, t):
                dve.wait_ge(b_logit.sem, b_logit.at(g))
                if started(g):
                    dve.wait_ge(b_res.sem, b_res.at(g - U))
                for j in range(J):
                    last = v.scalar_tensor_tensor(logit[:, s, j, :], psum2(4 + s % 2)[:, j, :],
                                                  dinv[:, bass.ds(g, 1), j], b0_row[:, :], ALU.mult, ALU.add)
                last.then_inc(b_max.sem, 1)
                dve.wait_ge(b_max.sem, b_max.at(g, 1))
                v.tensor_reduce(soft[:, 0, s, :], logit[:, s, :, :], AXX, ALU.max, negate=True
                                ).then_inc(b_max.sem, 1)

            def residual(g, s, t):
                dve.wait_ge(b_exp.sem, b_exp.at(g))
                if started(g, 2):
                    dve.wait_ge(b_out.sem, b_out.at(g - 2))
                v.tensor_tensor(soft[:, 0, s, :], soft[:, 0, s, :], soft[:, 2, s, :], ALU.subtract
                                ).then_inc(b_res.sem, 1)
                dve.wait_ge(b_res.sem, b_res.at(g, 1))
                for j in range(J):
                    last = v.scalar_tensor_tensor(ring_z[:, s % 2, j, :], logit[:, s, j, :],
                                                  soft[:, 0, s, j:j + 1], ring_a[:, U + s, j, :],
                                                  ALU.add, ALU.add)
                last.then_inc(b_res.sem, 1)
                dve.wait_ge(b_res.sem, b_res.at(g, 2))
                norm_stats(dve, b_norm, g, s, ring_z[:, s % 2, :, :])

            rounds(dve, NG, [(0, add), (1, bias), (2, residual), (3, lambda g, s, t: norm_refine(dve, b_norm, g, s))])

        def sgc_pe(pe):
            def up_(g, s, t):
                pe.wait_ge(b_sum.sem, b_sum.at(g))
                if started(g, 2):
                    pe.wait_ge(b_feat.sem, b_feat.at(g - 2))
                turn_rows(mix[:, s % 2, :, :], bank[2 + s % 2]).then_inc(b_up.sem, 1)

            def mul(g, s, t):
                pe.wait_ge(b_feat.sem, b_feat.at(g))
                if started(g, 2):
                    pe.wait_ge(b_max.sem, b_max.at(g - 2, 1))
                times(bank[4 + s % 2], [(feat[0][:, s % 2, :, :], w0t)]).then_inc(b_logit.sem, 1)
            rounds(pe, NG, [(0, up_), (1, mul)])

        def sgc_act(act):
            a = nc.scalar

            def copy(g, s, t):
                act.wait_ge(b_up.sem, b_up.at(g))
                if started(g, 2):
                    act.wait_ge(b_logit.sem, b_logit.at(g - 2))
                a.activation(feat[0][:, s % 2, :, :].rearrange("p h n -> p (h n)"), bank[2 + s % 2][:, :],
                             ACT.Copy).then_inc(b_feat.sem, 1)

            def expo(g, s, t):
                act.wait_ge(b_max.sem, b_max.at(g))
                if started(g, 1):
                    act.wait_ge(b_exp.sem, b_exp.at(g - 1))
                for j in range(J):
                    last = a.activation(junk[:, j, :], logit[:, s, j, :], ACT.Exp, bias=soft[:, 0, s, j:j + 1],
                                        accum_out=soft[:, 1, s, j:j + 1])
                last.then_inc(b_exp.sem, 1)
                act.wait_ge(b_exp.sem, b_exp.at(g, 1))
                a.activation(soft[:, 2, s, :], soft[:, 1, s, :], ACT.Ln).then_inc(b_exp.sem, 1)

            def result(g, s, t):
                if started(g):
                    act.wait_ge(stored[s], stores(1, t - 1))
                norm_apply(act, b_norm, g, s, ring_o[:, s, :, :], ring_z[:, s % 2, :, :], b_out)
            rounds(act, NG, [(0, copy), (1, expo), (2, lambda g, s, t: norm_roots(act, b_norm, g, s)), (3, result)])

        c_mean = Count(sem("c_mean"))
        c_up = Count(sem("c_up"), 2)
        c_feat = Count(sem("c_feat"), 2)
        c_mul = Count(sem("c_mul"))
        c_res = Count(sem("c_res"), 2)
        c_out = Count(sem("c_out"))
        c_up2 = Count(sem("c_up2"))
        c_feat2 = Count(sem("c_feat2"))
        c_proj = Count(sem("c_proj"))
        c_xp = Count(sem("c_xp"))
        c_sc = Count(sem("c_sc"))
        c_norm = norm_counts("c_norm")

        def sage_sync(sp):
            def load(g, s, t):
                if started(g):
                    sp.wait_ge(c_res.sem, c_res.at(g - U))
                    sp.sem_inc(held, 1)
                    sp.wait_ge(c_up.sem, c_up.at(g - U))
                    sp.sem_inc(held, 1)
                    sp.wait_ge(c_mean.sem, c_mean.at(g - U))
                    sp.sem_inc(held, 1)
                fetch(sp, x1, g, ring_a, s, s)
                fetch(sp, sums, g, ring_s, s, s)

            def store(g, s, t):
                sp.wait_ge(c_out.sem, c_out.at(g))
                sp.sem_inc(held, 1)
                sp.wait_ge(c_xp.sem, c_xp.at(g))
                sp.sem_inc(held, 1)
                sp.wait_ge(c_sc.sem, c_sc.at(g))
                sp.sem_inc(held, 1)
                put_out(sp, x2, g, ring_o, s)
                put_out(sp, xp, g, ring_b, s)
                put_out(sp, a16, g, scores, s)

            sums_complete(sp, 2)
            rounds(sp, NG, [(0, load), (5, store)], U, peel=True)
            step_complete(sp, 2)

        def sage_dve(dve):
            v = nc.vector

            def mean(g, s, t):
                dve.wait_ge(loaded[s], loads(2, t))
                if started(g, 2):
                    dve.wait_ge(c_up.sem, c_up.at(g - 2))
                for j in range(J):
                    last = v.tensor_scalar(mix[:, s % 2, j, :], ring_s[:, s, j, 0:D], rdeg[:, bass.ds(g, 1), j],
                                           None, ALU.mult)
                last.then_inc(c_mean.sem, 1)

            def residual(g, s, t):
                dve.wait_ge(c_mul.sem, c_mul.at(g))
                if started(g, 2):
                    dve.wait_ge(c_out.sem, c_out.at(g - 2))
                z = ring_z[:, s % 2, :, :]
                v.tensor_tensor(z, psum2(4), row2(b1_row), ALU.add).then_inc(c_res.sem, 1)
                dve.wait_ge(c_res.sem, c_res.at(g, 1))
                v.scalar_tensor_tensor(flat(z), flat(z), 0.0, flat(ring_a[:, s, :, :]), ALU.max, ALU.add
                                       ).then_inc(c_res.sem, 1)
                dve.wait_ge(c_res.sem, c_res.at(g, 2))
                norm_stats(dve, c_norm, g, s, z)

            def scores_out(g, s, t):
                dve.wait_ge(c_proj.sem, c_proj.at(g))
                if started(g):
                    dve.wait_ge(stored[s], stores(2, t - 1))
                v.tensor_copy(scores[:, s, :, :], bank[7][:, 0:4 * HEADS].rearrange("p (j h) -> p j h", j=J)
                              ).then_inc(c_sc.sem, 1)
            rounds(dve, NG, [(0, mean), (1, residual), (2, lambda g, s, t: norm_refine(dve, c_norm, g, s)),
                             (4, scores_out)])

        def sage_pe(pe):
            def up_(g, s, t):
                pe.wait_ge(loaded[s], loads(2, t))
                if started(g, 1):
                    pe.wait_ge(c_feat.sem, c_feat.at(g - 1))
                turn_rows(ring_a[:, s, :, :], bank[2]).then_inc(c_up.sem, 1)
                pe.wait_ge(c_mean.sem, c_mean.at(g))
                turn_rows(mix[:, s % 2, :, :], bank[3]).then_inc(c_up.sem, 1)

            def mul(g, s, t):
                pe.wait_ge(c_feat.sem, c_feat.at(g))
                if started(g, 1):
                    pe.wait_ge(c_res.sem, c_res.at(g - 1, 1))
                times(bank[4], [(feat[0][:, s % 2, :, :], w_self), (feat[1][:, s % 2, :, :], w_neigh)]
                      ).then_inc(c_mul.sem, 1)

            def up2(g, s, t):
                pe.wait_ge(c_out.sem, c_out.at(g))
                if started(g, 1):
                    pe.wait_ge(c_feat2.sem, c_feat2.at(g - 1))
                turn_rows(ring_o[:, s, :, :], bank[5]).then_inc(c_up2.sem, 1)

            def project(g, s, t):
                pe.wait_ge(c_feat2.sem, c_feat2.at(g))
                if started(g, 1):
                    pe.wait_ge(c_xp.sem, c_xp.at(g - 1))
                    pe.wait_ge(c_sc.sem, c_sc.at(g - 1))
                f = hid[:, s % 2, :, :]
                times(bank[6], [(f, w_gat)])
                times(bank[7], [(f, w_att)], 2 * HEADS).then_inc(c_proj.sem, 1)
            rounds(pe, NG, [(0, up_), (1, mul), (3, up2), (4, project)])

        def sage_act(act):
            a = nc.scalar

            def copy(g, s, t):
                for k in range(2):
                    act.wait_ge(c_up.sem, c_up.at(g, k + 1))
                    if started(g, 2) and k == 0:
                        act.wait_ge(c_mul.sem, c_mul.at(g - 2))
                    a.activation(feat[k][:, s % 2, :, :].rearrange("p h n -> p (h n)"), bank[2 + k][:, :],
                                 ACT.Copy).then_inc(c_feat.sem, 1)

            def result(g, s, t):
                if started(g):
                    act.wait_ge(stored[s], stores(2, t - 1))
                norm_apply(act, c_norm, g, s, ring_o[:, s, :, :], ring_z[:, s % 2, :, :], c_out)

            def copy2(g, s, t):
                act.wait_ge(c_up2.sem, c_up2.at(g))
                if started(g, 2):
                    act.wait_ge(c_proj.sem, c_proj.at(g - 2))
                a.activation(hid[:, s % 2, :, :].rearrange("p h n -> p (h n)"), bank[5][:, :],
                             ACT.Copy).then_inc(c_feat2.sem, 1)

            def xp_out(g, s, t):
                act.wait_ge(c_proj.sem, c_proj.at(g))
                if started(g):
                    act.wait_ge(stored[s], stores(2, t - 1))
                a.activation(flat(ring_b[:, s, :, :]), bank[6][:, :], ACT.Copy).then_inc(c_xp.sem, 1)
            rounds(act, NG, [(0, copy), (1, lambda g, s, t: norm_roots(act, c_norm, g, s)), (2, result),
                             (3, copy2), (4, xp_out)])

        d_own = Count(sem("d_own"), 4)
        d_pow = Count(sem("d_pow"))
        d_den = Count(sem("d_den"), 4)
        d_mix = Count(sem("d_mix"), 4)
        d_nrm = Count(sem("d_nrm"))
        d_up = Count(sem("d_up"))
        d_feat = Count(sem("d_feat"))
        d_hid = Count(sem("d_hid"))
        d_relu = Count(sem("d_relu"))
        d_mul = Count(sem("d_mul"))
        d_res = Count(sem("d_res"), 2)
        d_out = Count(sem("d_out"))
        d_norm1 = norm_counts("d_norm1", 0)
        d_norm2 = norm_counts("d_norm2", 1)

        def gat_sync(sp):
            def load(g, s, t):
                if started(g):
                    sp.wait_ge(d_mix.sem, d_mix.at(g - U))
                    sp.sem_inc(held, 1)
                if started(g, RA):
                    sp.wait_ge(d_res.sem, d_res.at(g - RA))
                    sp.sem_inc(held, 1)
                fetch(sp, x2, g, ring_a, s, s % U)
                fetch(sp, xp, g, ring_b, s % U, s % U)
                fetch(sp, sums_gat, g, ring_s, s % U, s % U, XW)
                fetch(sp, a16, g, scores, s % U, s % U, 2 * HEADS)

            def store(g, s, t):
                sp.wait_ge(d_out.sem, d_out.at(g))
                sp.sem_inc(held, 1)
                put_out(sp, x3, g, ring_o, s % U)

            sums_complete(sp, 3)
            rounds(sp, NG, [(0, load), (7, store)], RA, peel=True)
            step_complete(sp, 3)

        def round_u(g, s, t):
            return t * 2 + (s // U)

        def gat_dve(dve):
            v = nc.vector

            def own(g, s8, t8):
                s, t = s8 % U, round_u(g, s8, t8)
                dve.wait_ge(loaded[s], loads(3, t))
                if started(g):
                    dve.wait_ge(d_den.sem, d_den.at(g - U))
                a_s, a_d = scores[:, s, :, 0:HEADS], scores[:, s, :, HEADS:]
                e = small[:, s, 0, :].rearrange("p (j h) -> p j h", j=J)
                v.tensor_tensor(e, a_s, a_d, ALU.add).then_inc(d_own.sem, 1)
                dve.wait_ge(d_own.sem, d_own.at(g, 1))
                v.scalar_tensor_tensor(e, e, 0.2, e, ALU.mult, ALU.max).then_inc(d_own.sem, 1)
                dve.wait_ge(d_own.sem, d_own.at(g, 2))
                v.tensor_tensor(e, e, ring_s[:, s, :, D + HEADS:XW], ALU.subtract).then_inc(d_own.sem, 1)
                dve.wait_ge(d_own.sem, d_own.at(g, 3))
                v.tensor_tensor(e, e, has_in[:, bass.ds(g, 1), :].rearrange("p g j -> p (g j)").unsqueeze(2)
                                .to_broadcast([P, J, HEADS]), ALU.mult).then_inc(d_own.sem, 1)

            def attend(g, s8, t8):
                s = s8 % U
                e, den, r, own_w = (small[:, s, q, :].rearrange("p (j h) -> p j h", j=J) for q in range(4))
                dve.wait_ge(d_pow.sem, d_pow.at(g))
                v.scalar_tensor_tensor(den, ring_s[:, s, :, D:D + HEADS], 1e-16, e, ALU.add, ALU.add
                                       ).then_inc(d_den.sem, 1)
                dve.wait_ge(d_den.sem, d_den.at(g, 1))
                v.reciprocal(r, den).then_inc(d_den.sem, 1)
                dve.wait_ge(d_den.sem, d_den.at(g, 2))
                v.tensor_tensor(own_w, e, r, ALU.mult).then_inc(d_den.sem, 1)
                if started(g, 2):
                    dve.wait_ge(d_nrm.sem, d_nrm.at(g - 2))
                by_head = "p j (h d) -> p j h d"
                sums_v = ring_s[:, s, :, 0:D].rearrange(by_head, d=HD)
                xp_v = ring_b[:, s, :, :].rearrange(by_head, d=HD)
                z = ring_z[:, s % 2, :, :]
                z_v = z.rearrange(by_head, d=HD)
                v.tensor_tensor(z_v, sums_v, r.unsqueeze(3).to_broadcast([P, J, HEADS, HD]), ALU.mult
                                ).then_inc(d_den.sem, 1)
                dve.wait_ge(d_den.sem, d_den.at(g, 4))
                v.tensor_tensor(xp_v, xp_v, own_w.unsqueeze(3).to_broadcast([P, J, HEADS, HD]), ALU.mult
                                ).then_inc(d_mix.sem, 1)
                dve.wait_ge(d_mix.sem, d_mix.at(g, 1))
                v.tensor_tensor(z, z, ring_b[:, s, :, :], ALU.add).then_inc(d_mix.sem, 1)
                dve.wait_ge(d_mix.sem, d_mix.at(g, 2))
                v.tensor_tensor(z, z, row2(gat_row), ALU.add).then_inc(d_mix.sem, 1)
                dve.wait_ge(d_mix.sem, d_mix.at(g, 3))
                v.tensor_tensor(z, z, ring_a[:, s8, :, :], ALU.add).then_inc(d_mix.sem, 1)
                dve.wait_ge(d_mix.sem, d_mix.at(g, 4))
                norm_stats(dve, d_norm1, g, s, z)

            def residual(g, s8, t8):
                s = s8 % U
                z = mlp_z[:, s % 2, :, :]
                dve.wait_ge(d_mul.sem, d_mul.at(g))
                if started(g, 2):
                    dve.wait_ge(d_out.sem, d_out.at(g - 2))
                v.tensor_tensor(z, psum2(6), row2(m2_row), ALU.add).then_inc(d_res.sem, 1)
                dve.wait_ge(d_res.sem, d_res.at(g, 1))
                v.tensor_tensor(z, z, ring_a[:, s8, :, :], ALU.add).then_inc(d_res.sem, 1)
                dve.wait_ge(d_res.sem, d_res.at(g, 2))
                norm_stats(dve, d_norm2, g, s, z)
            rounds(dve, NG, [(0, own), (1, attend), (2, lambda g, s, t: norm_refine(dve, d_norm1, g, s % U)),
                             (5, residual), (6, lambda g, s, t: norm_refine(dve, d_norm2, g, s % U))], RA)

        def gat_pe(pe):
            def up_(g, s, t):
                pe.wait_ge(d_nrm.sem, d_nrm.at(g))
                if started(g, 2):
                    pe.wait_ge(d_feat.sem, d_feat.at(g - 2))
                turn_rows(mix[:, s % 2, :, :], bank[2 + s % 2]).then_inc(d_up.sem, 1)

            def hidden(g, s, t):
                pe.wait_ge(d_feat.sem, d_feat.at(g))
                if started(g, 2):
                    pe.wait_ge(d_relu.sem, d_relu.at(g - 2))
                for f in range(2):
                    for h in range(2):
                        last = nc.tensor.matmul(bank[4 + s % 2][:, f * D:(f + 1) * D],
                                                w_m1[:, h, f * P:(f + 1) * P], feat[0][:, s % 2, h, :],
                                                start=h == 0, stop=h == 1)
                last.then_inc(d_hid.sem, 1)

            def mul(g, s, t):
                pe.wait_ge(d_relu.sem, d_relu.at(g))
                if started(g, 1):
                    pe.wait_ge(d_res.sem, d_res.at(g - 1, 1))
                times(bank[6], [(hid[:, s % 2, :, :], w_m2)]).then_inc(d_mul.sem, 1)
            rounds(pe, NG, [(3, up_), (4, hidden), (5, mul)])

        def gat_act(act):
            a = nc.scalar

            def power(g, s8, t8):
                s = s8 % U
                act.wait_ge(d_own.sem, d_own.at(g))
                a.activation(small[:, s, 0, :], small[:, s, 0, :], ACT.Exp).then_inc(d_pow.sem, 1)

            def normed(g, s8, t8):
                s = s8 % U
                if started(g, 2):
                    act.wait_ge(d_up.sem, d_up.at(g - 2))
                norm_apply(act, d_norm1, g, s, mix[:, s % 2, :, :], ring_z[:, s % 2, :, :], d_nrm)

            def copy(g, s, t):
                act.wait_ge(d_up.sem, d_up.at(g))
                if started(g, 2):
                    act.wait_ge(d_hid.sem, d_hid.at(g - 2))
                a.activation(feat[0][:, s % 2, :, :].rearrange("p h n -> p (h n)"), bank[2 + s % 2][:, :],
                             ACT.Copy).then_inc(d_feat.sem, 1)

            def relu(g, s, t):
                act.wait_ge(d_hid.sem, d_hid.at(g))
                if started(g, 2):
                    act.wait_ge(d_mul.sem, d_mul.at(g - 2))
                for f in range(2):
                    last = a.activation(hid[:, s % 2, f, :], bank[4 + s % 2][:, f * D:(f + 1) * D], ACT.Relu,
                                        bias=m1_col[:, f:f + 1])
                last.then_inc(d_relu.sem, 1)

            def result(g, s8, t8):
                s = s8 % U
                if started(g):
                    act.wait_ge(stored[s], stores(3, round_u(g, s8, t8) - 1))
                norm_apply(act, d_norm2, g, s, ring_o[:, s, :, :], mlp_z[:, s % 2, :, :], d_out)
            rounds(act, NG, [(0, power), (1, lambda g, s, t: norm_roots(act, d_norm1, g, s % U)), (2, normed),
                             (3, copy), (4, relu), (5, lambda g, s, t: norm_roots(act, d_norm2, g, s % U)),
                             (6, result)], RA)

        mlp_z = feat[1][:, :, :, :].rearrange("p s h n -> p s (h n)").rearrange("p s (j d) -> p s j d", j=J)

        e_up = Count(sem("e_up"))
        e_feat = Count(sem("e_feat"))
        e_mul = Count(sem("e_mul"))
        e_res = Count(sem("e_res"), 2)
        e_out = Count(sem("e_out"))
        e_norm = norm_counts("e_norm")

        def gcn_sync(sp):
            def load(g, s, t):
                if started(g):
                    sp.wait_ge(e_res.sem, e_res.at(g - U))
                    sp.sem_inc(held, 1)
                    sp.wait_ge(e_up.sem, e_up.at(g - U))
                    sp.sem_inc(held, 1)
                fetch(sp, x3, g, ring_a, s, s)
                fetch(sp, sums_src, g, ring_s, s, s)

            def store(g, s, t):
                sp.wait_ge(e_out.sem, e_out.at(g))
                sp.sem_inc(held, 1)
                put_out(sp, out, g, ring_o, s)

            sums_complete(sp, 4)
            rounds(sp, NG, [(0, load), (3, store)], U, peel=True)
            step_complete(sp, 4)

        def gcn_dve(dve):
            v = nc.vector

            def residual(g, s, t):
                z = ring_z[:, s % 2, :, :]
                dve.wait_ge(e_mul.sem, e_mul.at(g))
                if started(g, 2):
                    dve.wait_ge(e_out.sem, e_out.at(g - 2))
                v.tensor_tensor(z, psum2(4 + s % 2), row2(l3_row), ALU.add).then_inc(e_res.sem, 1)
                dve.wait_ge(e_res.sem, e_res.at(g, 1))
                v.tensor_tensor(z, z, ring_a[:, s, :, :], ALU.add).then_inc(e_res.sem, 1)
                dve.wait_ge(e_res.sem, e_res.at(g, 2))
                norm_stats(dve, e_norm, g, s, z)
            rounds(dve, NG, [(1, residual), (2, lambda g, s, t: norm_refine(dve, e_norm, g, s))])

        def gcn_pe(pe):
            def up_(g, s, t):
                pe.wait_ge(loaded[s], loads(4, t))
                if started(g, 2):
                    pe.wait_ge(e_feat.sem, e_feat.at(g - 2))
                turn_rows(ring_s[:, s, :, 0:D], bank[2 + s % 2]).then_inc(e_up.sem, 1)

            def mul(g, s, t):
                pe.wait_ge(e_feat.sem, e_feat.at(g))
                if started(g, 2):
                    pe.wait_ge(e_res.sem, e_res.at(g - 2, 1))
                times(bank[4 + s % 2], [(feat[0][:, s % 2, :, :], w_l3)]).then_inc(e_mul.sem, 1)
            rounds(pe, NG, [(0, up_), (1, mul)])

        def gcn_act(act):
            def copy(g, s, t):
                act.wait_ge(e_up.sem, e_up.at(g))
                if started(g, 2):
                    act.wait_ge(e_mul.sem, e_mul.at(g - 2))
                nc.scalar.activation(feat[0][:, s % 2, :, :].rearrange("p h n -> p (h n)"), bank[2 + s % 2][:, :],
                                     ACT.Copy).then_inc(e_feat.sem, 1)

            def result(g, s, t):
                if started(g):
                    act.wait_ge(stored[s], stores(4, t - 1))
                norm_apply(act, e_norm, g, s, ring_o[:, s, :, :], ring_z[:, s % 2, :, :], e_out)
            rounds(act, NG, [(0, copy), (1, lambda g, s, t: norm_roots(act, e_norm, g, s)), (2, result)])

        block = ctx.enter_context(nc.Block())

        @block.sync
        def _(sp):
            weights_sync(sp)
            sort_sync(sp)
            sp.sem_inc(tables_done, 1)
            hop_sync(sp)
            sgc_sync(sp)
            sage_sync(sp)
            gat_sync(sp)
            gcn_sync(sp)

        @block.gpsimd
        def _(pool):
            sort_pool(pool)
            for run in range(RUNS):
                if run == 3:
                    attention_pool(pool)
                edges_pool(pool, run)

        @block.vector
        def _(dve):
            nc.vector.memset(zero_w[:, :], 0.0).then_inc(zero_w_made, 1)
            sort_dve(dve)
            weights_vec(dve)
            for run, nodes in enumerate((hop_dve, sgc_dve, sage_dve, gat_dve, gcn_dve)):
                if run == 3:
                    attention_dve(dve)
                if run == 4:
                    make_same(dve, 1)
                edges_dve(dve, run)
                nodes(dve)

        @block.tensor
        def _(pe):
            sort_pe(pe)
            weights_tensor(pe)
            for run, nodes in enumerate((None, sgc_pe, sage_pe, gat_pe, gcn_pe)):
                if run == 3:
                    attention_pe(pe)
                if run == 4:
                    make_same_pe(pe, 1)
                edges_pe(pe, run)
                if nodes:
                    nodes(pe)

        @block.scalar
        def _(act):
            act.preload_act_table_set("natural_log_exp_and_others")
            act.wait_ge(zero_w_made, 1)
            sort_act(act)
            for run, nodes in enumerate((hop_act, sgc_act, sage_act, gat_act, gcn_act)):
                if run == 3:
                    attention_act(act)
                edges_act(act, run)
                nodes(act)


_INS = ['x', 'src', 'dst', 'edge_weight', 'L0_gnn_W', 'L0_gnn_b', 'L1_gnn_W_self', 'L1_gnn_W_neigh', 'L1_gnn_b',
        'L2_gnn_W', 'L2_gnn_att_src', 'L2_gnn_att_dst', 'L2_gnn_bias', 'L2_gnn_ln_g', 'L2_gnn_ln_b',
        'L2_gnn_W1', 'L2_gnn_b1', 'L2_gnn_W2', 'L2_gnn_b2', 'L3_gnn_weight', 'L3_gnn_bias']


def kernel(**inputs):
    import numpy as _np
    import concourse.bacc as _bacc
    from concourse import mybir as _mybir
    from concourse.bass_utils import run_bass_kernel_spmd as _run

    nc = _bacc.Bacc("TRN2", target_bir_lowering=False, num_devices=1)
    arrays, args = {}, []
    for name in _INS:
        a = _np.ascontiguousarray(inputs[name])
        arrays[f"in_{name}_dram"] = a
        args.append(nc.dram_tensor(f"in_{name}_dram", a.shape, _mybir.dt.from_np(a.dtype), kind="ExternalInput").ap())
    out = nc.dram_tensor("out_0_dram", (50000, 256), _mybir.dt.float32, kind="ExternalOutput").ap()
    gnn_program(nc, *args, out)
    r = _run(nc, [arrays], core_ids=[0])
    return r.results[0]["out_0_dram"]
```

```python
import concourse.bass as bass
from concourse import mybir
from contextlib import ExitStack

F32 = mybir.dt.float32
BF16 = mybir.dt.bfloat16
I32 = mybir.dt.int32
ALU = mybir.AluOpType
ACT = mybir.ActivationFunctionType
AXX = mybir.AxisListType.X

P = 128
N = 50000
E = 25000
D = 256
HEADS = 8
HD = D // HEADS
RADIX = 256
HIGH = -(-N // RADIX)
NPAD = HIGH * RADIX
PAD = NPAD - 1

J = 2
GROUP = J * P
NG = NPAD // GROUP
LAST = (N - (NG - 1) * GROUP) // J
U = 4

IC = -(-E // P)
IH = IC // 2
EC = P - 1
NC = 200
BIG = 1.0e30
FAR = 1 << 20
XW = D + 2 * HEADS


def rounds(eng, n, stages, u=U, lead=None, peel=False):
    deep = max(max(lag) if isinstance(lag, tuple) else lag for lag, _ in stages)
    lead = lead or u * (1 + -(-max(deep, 1) // u))
    end = n // u * u - (u if peel else 0)

    def step(i):
        for lag, f in stages:
            if isinstance(lag, tuple):
                f(*((i - k, (i - k) % u, (i - k) // u) if 0 <= i - k < n else None for k in lag))
            elif 0 <= i - lag < n:
                f(i - lag, (i - lag) % u, (i - lag) // u)

    for i in range(lead):
        step(i)
    with eng.Fori(lead // u, end // u) as r:
        for k in range(u):
            for lag, f in stages:
                if isinstance(lag, tuple):
                    f(*((r * u + (k - q), (k - q) % u, r + (k - q) // u) for q in lag))
                else:
                    f(r * u + (k - lag), (k - lag) % u, r + (k - lag) // u)
    for i in range(end, n + deep):
        step(i)


def started(g, n=U):
    return not isinstance(g, int) or g >= n


class Count:

    def __init__(self, sem, per=1, total=0):
        self.sem, self.per, self.total = sem, per, total

    def at(self, g, k=None, run=0):
        return g * self.per + (run * self.total * self.per + (self.per if k is None else k))


def gnn_program(nc, x, src, dst, edge_weight, W0, b0, Wself, Wneigh, b1, Wg, att_src, att_dst,
                gat_bias, ln_g, ln_b, Wm1, bm1, Wm2, bm2, Wl3, bl3, out):
    ctx = ExitStack()
    with ctx:
        def sem(name):
            return ctx.enter_context(nc.semaphore(name))

        def sb(name, shape, dt=F32, where=ctx):
            return where.enter_context(nc.sbuf_tensor(name, shape, dt))

        def pb(name, shape, where=ctx):
            return where.enter_context(nc.psum_tensor(name, shape, F32))

        ident = sb("ident", [P, P])
        flip = sb("flip", [P, P])
        ident_b = sb("ident_b", [P, P], BF16)
        flip_b = sb("flip_b", [P, P], BF16)
        ones_f = sb("ones_f", [P, P])
        ones_b = sb("ones_b", [P, P], BF16)
        before = sb("before", [P, P], BF16)
        upto = sb("upto", [P, P], BF16)
        counting = sb("counting", [P, RADIX], BF16)
        zero_w = sb("zero_w", [1, XW])
        not0 = sb("not0", [P, 1])
        is0 = sb("is0", [P, 1])
        neg0 = sb("neg0", [P, 1])

        at = [sb(f"at{o}", [P, NC, 3], I32) for o in range(2)]
        key_in = [sb(f"key_in{o}", [P, NC]) for o in range(2)]
        key_out = [sb(f"key_out{o}", [P, NC]) for o in range(2)]
        weight = sb("weight", [P, NC])
        gate_fwd = sb("gate_fwd", [P, NC])
        gate_bwd = sb("gate_bwd", [P, NC])
        first = sb("first", [P, NC])
        diag = sb("diag", [P, 2, 4, P])
        same = sb("same", [P, NC, P], BF16)
        dinv = sb("dinv", [P, NG, J])
        dinv2 = sb("dinv2", [P, NG, J])
        rdeg = sb("rdeg", [P, NG, J])
        has_in = sb("has_in", [P, NG, J])

        def table(name, shape):
            return nc.dram_tensor(name, shape, F32, kind="Internal").ap()

        deg_tab = table("deg_tab", (NPAD, 1))
        dinv_tab = table("dinv_tab", (NPAD, 1))
        sums = table("sums", (NPAD, D))
        sums_gat = table("sums_gat", (NPAD, XW))
        sums_src = table("sums_src", (NPAD, D))
        y1 = table("y1", (NPAD, D))
        x1 = table("x1", (NPAD, D))
        x2 = table("x2", (NPAD, D))
        x3 = table("x3", (NPAD, D))
        xp = table("xp", (NPAD, D))
        a16 = table("a16", (NPAD, 2 * HEADS))
        bank = [pb(f"bank{i}", [P, 512]) for i in range(8)]

        def square(name, t=2, w=D):
            return sb(name, [P, t, w])
        w0t, w_self, w_neigh, w_gat, w_m1, w_m2, w_l3 = (
            square(n) for n in ("w0t", "w_self", "w_neigh", "w_gat", "w_m1", "w_m2", "w_l3"))
        w_att = square("w_att", 2, 2 * HEADS)
        rows = {n: sb(n, [P, D]) for n in ("b0_row", "b1_row", "gat_row", "m2_row", "l3_row")}
        b0_row, b1_row, gat_row, m2_row, l3_row = rows.values()
        m1_col = sb("m1_col", [P, 2])

        tmp = ExitStack()
        raw = [sb(f"raw{a}", [IH, 2, P], I32, tmp) for a in range(2)]
        raw_w = sb("raw_w", [IH, 2, P], F32, tmp)
        digit_i = sb("digit_i", [IH, 4, 2, P], I32, tmp)
        digit_f = sb("digit_f", [IH, 4, 2, P], F32, tmp)
        part = sb("part", [P, 7, IC], F32, tmp)
        part_b = sb("part_b", [P, IC], BF16, tmp)
        parts_of = ([0, 1, 2, 3], [2, 3, 0, 1, 4, 5, 6])
        moved = [sb(f"moved{o}", [P, len(parts_of[o]), NC], F32, tmp) for o in range(2)]
        hot = [sb(f"hot{o}", [P, U, RADIX + HIGH], BF16, tmp) for o in range(2)]
        base = [sb(f"base{o}", [P, RADIX + HIGH], F32, tmp) for o in range(2)]
        nought = sb("nought", [P, RADIX], F32, tmp)
        picked_row = sb("picked_row", [P, 2, RADIX], BF16, tmp)
        pos = [sb(f"pos{o}", [P, IC], F32, tmp) for o in range(2)]
        pos_i = [sb(f"pos_i{o}", [P, 3, IC], I32, tmp) for o in range(2)]
        row_of = [sb(f"row_of{o}", [P, IC], F32, tmp) for o in range(2)]
        col_of = [sb(f"col_of{o}", [P, IC], F32, tmp) for o in range(2)]
        wrap = sb("wrap", [P, 2, IC], F32, tmp)
        hot_row = [sb(f"hot_row{o}", [P, 2, len(parts_of[o]), P], BF16, tmp) for o in range(2)]
        apart = sb("apart", [P, U, RADIX], BF16, tmp)
        plain_row = sb("plain_row", [P, 2, P], BF16, tmp)
        hot_col = [sb(f"hot_col{o}", [P, 2, NC], BF16, tmp) for o in range(2)]
        slot_at = sb("slot_at", [P, NC], F32, tmp)
        key = [sb(f"key{o}", [P, NC + 2], F32, tmp) for o in range(2)]
        other = sb("other", [P, NC], F32, tmp)
        nxt = sb("nxt", [P, NC], F32, tmp)
        work = sb("work", [P, 2, NC], F32, tmp)
        stay = sb("stay", [P, P], F32, tmp)
        wrap_in = sb("wrap_in", [P, P], F32, tmp)
        up = sb("up", [P, P], F32, tmp)
        up_wrap = sb("up_wrap", [P, P], F32, tmp)
        down = sb("down", [P, P], F32, tmp)
        down_wrap = sb("down_wrap", [P, P], F32, tmp)
        indeg = sb("indeg", [IH, 2, RADIX], F32, tmp)
        deg = sb("deg", [IH, 2, RADIX], F32, tmp)
        dinv_n = sb("dinv_n", [IH, 2, RADIX], F32, tmp)
        newton = sb("newton", [IH, 2, RADIX], F32, tmp)
        zero_row = sb("zero_row", [P, XW * NPAD // (P * 49)], F32, tmp)

        held = sem("held")
        consts = sem("consts")
        padded = sem("padded")
        edges_in = sem("edges_in")
        zeroed = sem("zeroed")
        setup_dve = sem("setup_dve")
        digits_up = sem("digits_up")
        hot_made = [Count(sem(f"hot_made{o}"), 1, IC) for o in range(2)]
        hot_counted = Count(sem("hot_counted"), 1, IC)
        base_in = Count(sem("base_in"), 1)
        ranked = Count(sem("ranked"), 2, IC)
        picked = Count(sem("picked"), 2, IC)
        folded = Count(sem("folded"), 1, IC)
        squared = Count(sem("squared"), 1, IC)
        spread = Count(sem("spread"), 2, IC)
        valued = Count(sem("valued"), 1, IC)
        valued_pool = Count(sem("valued_pool"), 1, IC)
        placed = Count(sem("placed"), 1, IC)
        ready_pass = sem("ready_pass")
        ready_move = sem("ready_move")
        lnout = sem("lnout")
        turned = sem("turned")
        table_out = sem("table_out")
        diag_made = [Count(sem(f"diag_made{o}"), 1, NC // 4) for o in range(2)]
        keys_wide = [Count(sem(f"keys_wide{o}"), 1, NC // 4) for o in range(2)]
        same_made = [Count(sem(f"same_made{o}"), 1, NC // 4) for o in range(2)]

        ACT_PARTS, POOL_PARTS = range(0, 4), range(4, 7)
        DIGITS_READY = 4 + 1 + 8

        def sort_sync(sp):
            sp.wait_ge(padded, 1)
            full = (E // P - IH)
            for a, (to, of) in enumerate(((raw[0], dst), (raw[1], src), (raw_w, edge_weight))):
                sp.dma_start(to[:, 0, :], of[0:IH * P].rearrange("(r k) -> r k", k=P)).then_inc(edges_in, 16)
                sp.dma_start(to[0:full, 1, :],
                             of[IH * P:(IH + full) * P].rearrange("(r k) -> r k", k=P)).then_inc(edges_in, 16)
                sp.dma_start(to[full:full + 1, 1, 0:E % P],
                             of[(IH + full) * P:E].rearrange("(r k) -> r k", r=1)).then_inc(edges_in, 16)
            flat = [t.rearrange("(i p r) d -> i p (r d)", i=49, p=P) for t in (sums, sums_gat, sums_src)]
            with sp.Fori(0, 49) as i:
                for t in flat:
                    w = t.shape[-1]
                    sp.dma_start(t[bass.ds(i, 1), :, :].rearrange("i p w -> p (i w)"),
                                 zero_row[:, 0:w]).then_inc(zeroed, 16)
            sp.wait_ge(lnout, 3)
            sp.dma_start(dinv_tab.rearrange("(h r l) o -> r h (l o)", h=2, l=RADIX),
                         dinv_n[:, :, :]).then_inc(table_out, 16)
            sp.wait_ge(table_out, 16)
            sp.wait_ge(zeroed, 16 * 49 * 3)

        def sort_digit(q, o, g):
            return part[:, 2 * o, bass.ds(g, 1)] if q == 0 else moved[o][:, 1, bass.ds(g, 1)]

        def value(q, o, k, g):
            return part[:, parts_of[o][k], bass.ds(g, 1)] if q == 0 else moved[o][:, k, bass.ds(g, 1)]

        def sort_pool(pool):
            for t in (ident, flip, stay, wrap_in, up, up_wrap, down, down_wrap):
                nc.gpsimd.memset(t[:, :], 0.0)
            nc.gpsimd.memset(before[:, :], 1.0)
            nc.gpsimd.memset(not0[:, :], 1.0)
            nc.gpsimd.memset(is0[:, :], 0.0).then_inc(consts, 1)
            nc.gpsimd.memset(neg0[:, :], 0.0).then_inc(consts, 1)
            pool.wait_ge(consts, 2)

            def put(t, base_v, cm, pat, op=ALU.not_equal, fill=1.0):
                return nc.gpsimd.affine_select(out=t, in_=t, pattern=pat, compare_op=op, fill=fill,
                                               base=base_v, channel_multiplier=cm)
            put(ident[:, :], 0, 1, [[-1, P]])
            put(flip[:, :], 1 - P, 1, [[1, P]])
            put(stay[:, 1:P], -1, 1, [[-1, P - 1]])
            put(wrap_in[:, 0:1], 1 - P, 1, [[0, 1]])
            put(up[:, :], -1, 1, [[-1, P]])
            put(up_wrap[:, P - 1:P], -1, 1, [[0, 1]])
            put(down[:, 2:P], -1, 1, [[-1, P - 2]])
            put(down_wrap[:, 1:2], 1 - P, 1, [[0, 1]])
            put(before[:, :], 0, -1, [[1, P]], ALU.is_gt, 0.0)
            put(not0[:, :], 0, 1, [[0, 1]], ALU.not_equal, 0.0)
            put(is0[:, :], 0, 1, [[0, 1]], ALU.not_equal, 1.0)
            put(neg0[:, :], 0, 1, [[0, 1]], ALU.not_equal, -BIG).then_inc(consts, 1)
            nc.gpsimd.iota(counting[:, :], [[1, RADIX]], base=0, channel_multiplier=0,
                           allow_small_or_imprecise_dtypes=True)
            nc.gpsimd.iota(slot_at[:, :], [[EC, NC]], base=-1, channel_multiplier=1,
                           allow_small_or_imprecise_dtypes=True).then_inc(consts, 1)

            for q in range(2):
                def rows_times_values(g, s, t, q=q):
                    s = s % 2
                    pool.wait_ge(spread.sem, spread.at(g, 1, run=q))
                    if started(g, 2):
                        pool.wait_ge(placed.sem, placed.at(g - 2, run=q))
                    pool.sem_inc(held, 1)
                    for k in POOL_PARTS:
                        last = nc.gpsimd.tensor_tensor(hot_row[1][:, s, k, :], plain_row[:, s, :],
                                                       value(q, 1, k, g).to_broadcast([P, P]), ALU.mult)
                    last.then_inc(valued_pool.sem, 1)
                rounds(pool, IC, [(0, rows_times_values)])

        def sort_dve(dve):
            v = nc.vector
            n_line = [0]

            def line(ins):
                n_line[0] += 1
                ins.then_inc(setup_dve, 1)
                dve.wait_ge(setup_dve, n_line[0])

            v.memset(zero_row[:, :], 0.0)
            v.memset(raw[0][:, :, :], PAD)
            v.memset(raw[1][:, :, :], PAD)
            v.memset(raw_w[:, :, :], 0.0).then_inc(padded, 1)
            v.memset(nought[:, :], 0.0)
            v.memset(ones_f[:, :], 1.0)
            v.memset(ones_b[:, :], 1.0)
            for o in range(2):
                v.memset(key[o][:, :], -1.0)
            dve.wait_ge(consts, 4)
            v.tensor_copy(ident_b[:, :], ident[:, :])
            v.tensor_copy(flip_b[:, :], flip[:, :])
            line(v.tensor_scalar(upto[:, :], before[:, :], -1.0, 1.0, ALU.mult, ALU.add))
            dve.wait_ge(edges_in, 16 * 9)
            for a in range(2):
                v.tensor_scalar(digit_i[:, 2 * a, :, :], raw[a][:, :, :], RADIX - 1, None, ALU.bitwise_and)
                line(v.tensor_scalar(digit_i[:, 2 * a + 1, :, :], raw[a][:, :, :], 8, None,
                                     ALU.logical_shift_right))
            line(v.tensor_copy(digit_f[:, :, :, :], digit_i[:, :, :, :]))
            dve.wait_ge(digits_up, 1)
            for b in range(2):
                v.tensor_copy(part[:, 2 * b:2 * b + 2, :],
                              bank[b][:, 0:2 * IC].rearrange("p (a c) -> p a c", a=2))
            line(v.tensor_copy(work[:, 0, 0:IC], bank[2][:, 0:IC]))
            for q in range(3):
                line(v.tensor_copy(part_b[:, :], work[:, q % 2, 0:IC]))
                line(v.tensor_copy(part[:, 4 + q, :], part_b[:, :]))
                if q < 2:
                    line(v.tensor_tensor(work[:, 1 - q % 2, 0:IC], work[:, q % 2, 0:IC],
                                         part[:, 4 + q, :], ALU.subtract))

            def one_hots(g, s, t):
                if started(g):
                    dve.wait_ge(hot_counted.sem, hot_counted.at(g - U))
                v.tensor_scalar(hot[0][:, s, 0:RADIX], counting[:, :],
                                part[:, 0, bass.ds(g, 1)], None, ALU.is_equal)
                for o in range(2):
                    last = v.tensor_scalar(hot[o][:, s, RADIX:], counting[:, 0:HIGH],
                                           part[:, 2 * o + 1, bass.ds(g, 1)], None, ALU.is_equal)
                last.then_inc(hot_made[0].sem, 1)
            rounds(dve, IC, [(0, one_hots)])

            dve.wait_ge(hot_counted.sem, hot_counted.at(IC - 1))
            for o in range(2):
                for lo, hi in ((0, RADIX), (RADIX, RADIX + HIGH)):
                    line(v.tensor_tensor_scan(base[o][:, lo:hi], nought[:, 0:hi - lo], bank[o][:, lo:hi],
                                              0.0, ALU.add, ALU.add))
                line(v.tensor_tensor(base[o][:, :], base[o][:, :], bank[o][:, 0:RADIX + HIGH], ALU.subtract))
            for h in range(2):
                line(v.tensor_copy(indeg[:, h, :], bank[2 + h][0:IH, 0:RADIX]))
            v.tensor_scalar(deg[:, :, :], indeg[:, :, :], 1.0, None, ALU.add).then_inc(ready_pass, 1)

            def newton_step(dve):
                dve.wait_ge(lnout, 2)
                line(v.tensor_tensor(newton[:, :, :], dinv_n[:, :, :], dinv_n[:, :, :], ALU.mult))
                line(v.tensor_tensor(newton[:, :, :], newton[:, :, :], deg[:, :, :], ALU.mult))
                line(v.tensor_scalar(newton[:, :, :], newton[:, :, :], -0.5, 1.5, ALU.mult, ALU.add))
                v.tensor_tensor(dinv_n[:, :, :], dinv_n[:, :, :], newton[:, :, :], ALU.mult).then_inc(lnout, 1)

            for q in range(2):
                width = (RADIX, HIGH)[q]
                cols = (IC, NC)[q]

                def hot_digit(g, s, t, q=q, width=width):
                    if started(g):
                        dve.wait_ge(folded.sem, folded.at(g - U, run=q))
                    v.tensor_scalar(hot[0][:, s, 0:width], counting[:, 0:width], sort_digit(q, 0, g),
                                    None, ALU.is_equal).then_inc(hot_made[0].sem, 1)

                def pick(g, s, t, q=q, width=width):
                    for o in range(2):
                        dve.wait_ge(ranked.sem, ranked.at(g, o + 1, run=q))
                        v.scalar_tensor_tensor(picked_row[:, o, 0:width], bank[o][:, 0:width], 1.0,
                                               hot[o][:, s, 0:width], ALU.mult, ALU.mult,
                                               accum_out=pos[o][:, bass.ds(g, 1)]).then_inc(picked.sem, 1)
                rounds(dve, IC, [(2, pick), (0, hot_digit)])
                dve.wait_ge(picked.sem, picked.at(IC - 1, run=q))

                for o in range(2):
                    line(v.tensor_copy(pos_i[o][:, 0, :], pos[o][:, :]))
                    line(v.tensor_scalar(pos_i[o][:, 1, :], pos_i[o][:, 0, :], 7, None,
                                         ALU.logical_shift_right))
                    line(v.tensor_scalar(pos_i[o][:, 2, :], pos_i[o][:, 0, :], P - 1, None, ALU.bitwise_and))
                    line(v.tensor_copy(col_of[o][:, :], pos_i[o][:, 1, :]))
                    line(v.tensor_copy(row_of[o][:, :], pos_i[o][:, 2, :]))
                    if q == 1:
                        line(v.tensor_tensor(row_of[o][:, :], row_of[o][:, :], col_of[o][:, :], ALU.add))
                        v.tensor_scalar(wrap[:, 0, :], row_of[o][:, :], float(EC), None, ALU.is_ge)
                        line(v.tensor_scalar(wrap[:, 1, :], row_of[o][:, :], float(2 * EC), None, ALU.is_ge))
                        line(v.tensor_tensor(wrap[:, 0, :], wrap[:, 0, :], wrap[:, 1, :], ALU.add))
                        line(v.tensor_tensor(col_of[o][:, :], col_of[o][:, :], wrap[:, 0, :], ALU.add))
                        line(v.tensor_scalar(wrap[:, 0, :], wrap[:, 0, :], -float(EC), 1.0, ALU.mult, ALU.add))
                        line(v.tensor_tensor(row_of[o][:, :], row_of[o][:, :], wrap[:, 0, :], ALU.add))
                if q == 0:
                    newton_step(dve)

                def spread_out(g, s, t, q=q, cols=cols):
                    s = s % 2
                    if started(g, 2):
                        dve.wait_ge(placed.sem, placed.at(g - 2, run=q))
                    v.tensor_scalar(plain_row[:, s, :], counting[:, 0:P], row_of[1][:, bass.ds(g, 1)],
                                    None, ALU.is_equal).then_inc(spread.sem, 1)
                    for o in range(2):
                        last = v.tensor_scalar(hot_col[o][:, s, 0:cols], counting[:, 0:cols],
                                               col_of[o][:, bass.ds(g, 1)], None, ALU.is_equal)
                    for k in range(len(parts_of[0])):
                        last = v.tensor_scalar(hot_row[0][:, s, k, :], counting[:, 0:P],
                                               row_of[0][:, bass.ds(g, 1)], value(q, 0, k, g),
                                               ALU.is_equal, ALU.mult)
                    last.then_inc(spread.sem, 1)
                rounds(dve, IC, [(0, spread_out)])
                dve.wait_ge(placed.sem, placed.at(IC - 1, run=q))
                for o in range(2):
                    n = len(parts_of[o])
                    for k in range(0, n, 2):
                        m = min(2, n - k)
                        last = v.tensor_copy(moved[o][:, k:k + m, 0:cols],
                                             bank[2 + 2 * o + k // 2][:, 0:m * cols]
                                             .rearrange("p (a c) -> p a c", a=m))
                line(last)
                dve.sem_inc(ready_pass, 1)

            line(v.tensor_scalar(work[:, 0, :], slot_at[:, :], float(E) - 0.5, None, ALU.is_le))
            line(v.tensor_scalar(work[:, 1, :], work[:, 0, :], -float(PAD), float(PAD), ALU.mult, ALU.add))
            for o in range(2):
                k_main = key[o][:, 1:NC + 1]
                line(v.scalar_tensor_tensor(k_main, moved[o][:, 1, :], float(RADIX), moved[o][:, 0, :],
                                            ALU.mult, ALU.add))
                line(v.tensor_tensor(k_main, k_main, work[:, 0, :], ALU.mult))
                line(v.tensor_tensor(k_main, k_main, work[:, 1, :], ALU.add))
                line(v.scalar_tensor_tensor(other[:, :], moved[o][:, 3, :], float(RADIX), moved[o][:, 2, :],
                                            ALU.mult, ALU.add))
                line(v.tensor_tensor(other[:, :], other[:, :], work[:, 0, :], ALU.mult))
                line(v.tensor_copy(at[o][:, :, 0], other[:, :]))
            line(v.tensor_tensor(weight[:, :], moved[1][:, 6, :], moved[1][:, 5, :], ALU.add))
            line(v.tensor_tensor(weight[:, :], weight[:, :], moved[1][:, 4, :], ALU.add))
            line(v.tensor_scalar(weight[:, :], weight[:, :], not0[:, 0:1], is0[:, 0:1], ALU.mult, ALU.add))
            dve.sem_inc(ready_pass, 1)
            for o in range(2):
                dve.wait_ge(turned, 2 + o)
                v.tensor_copy(key_in[o][:, :], bank[0][:, 0:NC])
                line(v.tensor_copy(key_out[o][:, :], bank[1][:, 0:NC]))
                line(v.tensor_copy(nxt[:, :], bank[2][:, 0:NC]))
                line(v.tensor_tensor(work[:, 0, :], key_out[o][:, :], nxt[:, :], ALU.is_equal))
                line(v.tensor_scalar(work[:, 0, :], work[:, 0, :], is0[:, 0:1], float(FAR), ALU.max, ALU.mult))
                line(v.tensor_tensor(work[:, 0, :], work[:, 0, :], key_out[o][:, :], ALU.add))
                line(v.tensor_copy(at[o][:, :, 1], work[:, 0, :]))
                if o == 0:
                    line(v.tensor_tensor(gate_bwd[:, :], key_out[0][:, :], nxt[:, :], ALU.not_equal))
                    line(v.tensor_scalar(gate_bwd[:, :], gate_bwd[:, :], not0[:, 0:1], -BIG,
                                         ALU.mult, ALU.mult))
                    line(v.tensor_tensor(first[:, :], key[0][:, 1:NC + 1], bank[3][:, 0:NC], ALU.not_equal))
                    line(v.tensor_scalar(first[:, :], first[:, :], not0[:, 0:1], None, ALU.mult))
                    line(v.tensor_scalar(gate_fwd[:, :], first[:, :], -BIG, None, ALU.mult))
                    line(v.tensor_scalar(work[:, 0, :], key[0][:, 1:NC + 1], float(N) - 0.5, not0[:, 0:1],
                                         ALU.is_le, ALU.mult))
                    line(v.tensor_tensor(work[:, 0, :], work[:, 0, :], key[0][:, 1:NC + 1], ALU.mult))
                    line(v.tensor_copy(at[0][:, :, 2], work[:, 0, :]))
                dve.sem_inc(ready_pass, 1)

            dve.wait_ge(turned, 4)
            line(v.tensor_copy(dinv[:, :, :], bank[4][:, 0:NG * J].rearrange("p (j g) -> p g j", j=J)))
            line(v.tensor_tensor(dinv2[:, :, :], dinv[:, :, :], dinv[:, :, :], ALU.mult))
            indeg_t = bank[5][:, 0:NG * J].rearrange("p (j g) -> p g j", j=J)
            line(v.tensor_scalar(rdeg[:, :, :], indeg_t, 1.0, None, ALU.max))
            line(v.reciprocal(rdeg[:, :, :], rdeg[:, :, :]))
            line(v.tensor_scalar(has_in[:, :, :], indeg_t, 1.0, None, ALU.min))
            make_same(dve, 0)

        def make_same(dve, o):
            v = nc.vector

            def spread_keys(g, s, t):
                s = s % 2
                if started(g, 2):
                    dve.wait_ge(keys_wide[o].sem, keys_wide[o].at(g - 2))
                v.tensor_tensor(diag[:, s, :, :], ident[:, :].unsqueeze(1).to_broadcast([P, 4, P]),
                                key_out[o][:, bass.ds(g * 4, 4)].unsqueeze(2).to_broadcast([P, 4, P]),
                                ALU.mult).then_inc(diag_made[o].sem, 1)

            def compare(g, s, t):
                s = s % 2
                dve.wait_ge(keys_wide[o].sem, keys_wide[o].at(g))
                v.tensor_tensor(same[:, bass.ds(g * 4, 4), :],
                                bank[6 + s][:, :].rearrange("p (c m) -> p c m", c=4),
                                key_in[o][:, bass.ds(g * 4, 4)].unsqueeze(2).to_broadcast([P, 4, P]),
                                ALU.is_equal).then_inc(same_made[o].sem, 1)
            rounds(dve, NC // 4, [(0, spread_keys), (1, compare)], 2)

        def make_same_pe(pe, o):
            def widen(g, s, t):
                s = s % 2
                pe.wait_ge(diag_made[o].sem, diag_made[o].at(g))
                if started(g, 2):
                    pe.wait_ge(same_made[o].sem, same_made[o].at(g - 2))
                nc.tensor.matmul(bank[6 + s][:, :], ones_f[:, :],
                                 diag[:, s, :, :].rearrange("p c m -> p (c m)"),
                                 start=True, stop=True).then_inc(keys_wide[o].sem, 1)
            rounds(pe, NC // 4, [(0, widen)], 2)

        def sort_pe(pe):
            m = nc.tensor
            pe.wait_ge(consts, 4)
            pe.wait_ge(edges_in, 16 * 9)
            pe.wait_ge(setup_dve, 4)
            for a in range(5):
                for h in range(2):
                    of = digit_f[:, a, h, :] if a < 4 else raw_w[:, h, :]
                    at = (a % 2) * IC + h * IH
                    last = m.transpose(bank[a // 2][:, at:at + IH], of, ident[0:IH, 0:IH])
            last.then_inc(digits_up, 1)

            def histogram(g, s, t):
                first_one = isinstance(g, int) and g == 0
                for o in range(2):
                    pe.wait_ge(hot_made[o].sem, hot_made[o].at(g))
                kw = dict(start=first_one, stop=True, skip_group_check=True)
                for o in range(2):
                    m.matmul(bank[o][:, 0:RADIX + HIGH], ones_b[:, :], hot[o][:, s, :], **kw)
                for h in range(2):
                    last = m.matmul(bank[2 + h][0:IH, 0:RADIX],
                                    hot[0][:, s, RADIX + h * IH:RADIX + (h + 1) * IH],
                                    hot[0][:, s, 0:RADIX], **kw)
                last.then_inc(hot_counted.sem, 1)
            pe.wait_ge(setup_dve, DIGITS_READY)
            rounds(pe, IC, [(0, histogram)])

            for q in range(2):
                width = (RADIX, HIGH)[q]
                cols = (IC, NC)[q]
                pe.wait_ge(ready_pass, 1 + q)
                for o in range(2):
                    m.matmul(bank[o][:, 0:width], ident[:, :],
                             base[o][:, q * RADIX:q * RADIX + width], start=True, stop=True,
                             skip_group_check=True)

                kw = dict(start=False, stop=True, skip_group_check=True)

                def rank(o, g, s, q=q, width=width, kw=kw):
                    pe.wait_ge(hot_made[o].sem, hot_made[o].at(g, run=q + 1))
                    m.matmul(bank[o][:, 0:width], before[:, :], hot[o][:, s, 0:width],
                             **kw).then_inc(ranked.sem, 1)

                def fold(o, g, s, q=q, width=width, kw=kw):
                    pe.wait_ge(picked.sem, picked.at(g, o + 1, run=q))
                    return m.matmul(bank[o][:, 0:width], upto[:, :], hot[o][:, s, 0:width], **kw)

                def rank_0(g, s, t, rank=rank):
                    rank(0, g, s)

                def fold_1(g, s, t, fold=fold):
                    fold(1, g, s).then_inc(folded.sem, 1)

                def rank_1_fold_0(g, s, t, rank=rank, fold=fold):
                    rank(1, g, s)
                    fold(0, g, s)
                rounds(pe, IC, [(0, rank_0), (1, fold_1), (0, rank_1_fold_0)])

                def place(g, s, t, q=q, cols=cols):
                    s = s % 2
                    pe.wait_ge(spread.sem, spread.at(g, run=q))
                    for o in range(2):
                        if o:
                            pe.wait_ge(valued.sem, valued.at(g, run=q))
                            pe.wait_ge(valued_pool.sem, valued_pool.at(g, run=q))
                        for k in range(len(parts_of[o])):
                            last = m.matmul(bank[2 + 2 * o + k // 2][:, k % 2 * cols:(k % 2 + 1) * cols],
                                            hot_row[o][:, s, k, :], hot_col[o][:, s, 0:cols],
                                            start=False, stop=True, skip_group_check=True)
                    last.then_inc(placed.sem, 1)
                for b in range(2, 8):
                    m.matmul(bank[b][:, 0:2 * cols], ident[:, :], zero_row[:, 0:2 * cols],
                             start=True, stop=True, skip_group_check=True)
                rounds(pe, IC, [(0, place)])

            pe.wait_ge(ready_pass, 4)
            for o in range(2):
                if o:
                    pe.wait_ge(ready_pass, 5)
                k = key[o]
                for b, pairs in enumerate((((stay, 1), (wrap_in, 0)), ((stay, 1), (wrap_in, 1)),
                                           ((up, 1), (up_wrap, 2)), ((down, 1), (down_wrap, 0)))):
                    for n, (shift, at) in enumerate(pairs):
                        last = m.matmul(bank[b][:, 0:NC], shift[:, :], k[:, at:at + NC],
                                        start=n == 0, stop=n == 1)
                last.then_inc(turned, 1 if o else 2)
            pe.wait_ge(lnout, 3)
            for b, t in ((4, dinv_n), (5, indeg)):
                for j in range(J):
                    for h in range(2):
                        last = m.transpose(bank[b][:, j * NG + h * IH:j * NG + (h + 1) * IH],
                                           t[:, h, j:RADIX:J], ident[0:IH, 0:IH])
            last.then_inc(turned, 1)
            make_same_pe(pe, 0)

        def sort_act(act):
            a = nc.scalar

            def distance(g, s, run, width, digit):
                if started(g):
                    act.wait_ge(hot_made[1].sem, hot_made[1].at(g - U, run=run))
                act.sem_inc(held, 1)
                a.activation(apart[:, s, 0:width], counting[:, 0:width], ACT.Square,
                             scale=-1.0, bias=digit).then_inc(squared.sem, 1)

            def nearest(g, s, run, width, reader):
                act.wait_ge(squared.sem, squared.at(g, run=run))
                if started(g):
                    act.wait_ge(reader.sem, reader.at(g - U, run=max(run - 1, 0)))
                a.activation(hot[1][:, s, 0:width], apart[:, s, 0:width], ACT.Relu, scale=-1.0,
                             bias=ones_f[:, 0:1]).then_inc(hot_made[1].sem, 1)

            act.wait_ge(setup_dve, DIGITS_READY)

            def low_distance(g, s, t):
                distance(g, s, 0, RADIX, sort_digit(0, 1, g))

            def low_nearest(g, s, t):
                nearest(g, s, 0, RADIX, hot_counted)
            rounds(act, IC, [(2, low_nearest), (0, low_distance)])

            act.wait_ge(ready_pass, 1)
            nc.scalar.activation(dinv_n[:, :, :], deg[:, :, :], ACT.Ln).then_inc(lnout, 1)
            act.wait_ge(lnout, 1)
            nc.scalar.activation(dinv_n[:, :, :], dinv_n[:, :, :], ACT.Exp, scale=-0.5).then_inc(lnout, 1)

            for q in range(2):
                width = (RADIX, HIGH)[q]

                def one_distance(g, s, t, q=q, width=width):
                    distance(g, s, q + 1, width, sort_digit(q, 1, g))

                def one_nearest(g, s, t, q=q, width=width):
                    nearest(g, s, q + 1, width, folded)
                act.wait_ge(ready_pass, 1 + q)
                rounds(act, IC, [(2, one_nearest), (0, one_distance)])

                def rows_times_values(g, s, t, q=q):
                    s = s % 2
                    act.wait_ge(spread.sem, spread.at(g, 1, run=q))
                    if started(g, 2):
                        act.wait_ge(placed.sem, placed.at(g - 2, run=q))
                    act.sem_inc(held, 1)
                    for k in ACT_PARTS:
                        last = nc.scalar.activation(hot_row[1][:, s, k, :], plain_row[:, s, :], ACT.Copy,
                                                    scale=value(q, 1, k, g))
                    last.then_inc(valued.sem, 1)
                rounds(act, IC, [(0, rows_times_values)])

        w0_in = sb("w0_in", [P, 2, D], F32, tmp)
        att_row = sb("att_row", [P, 2, D], F32, tmp)
        att_mul = sb("att_mul", [P, 2, D], F32, tmp)
        g_col = sb("g_col", [P, 2], F32, tmp)
        b_col = sb("b_col", [P, 2], F32, tmp)
        w_m1_in = sb("w_m1_in", [P, 2, D], F32, tmp)
        weights_in = sem("weights_in")
        weights_dve = sem("weights_dve")
        weights_pe = sem("weights_pe")
        N_WEIGHTS = 17

        def weights_sync(sp):
            def load(to, of):
                sp.dma_start(to, of).then_inc(weights_in, 16)
            for to, of in ((w0_in, W0), (w_self, Wself), (w_neigh, Wneigh), (w_gat, Wg),
                           (w_m1_in, Wm1), (w_m2, Wm2), (w_l3, Wl3)):
                load(to[:, :, :], of.rearrange("(t p) n -> p t n", p=P))
            for to, of in zip(rows.values(), (b0, b1, gat_bias, bm2, bl3)):
                load(to[:, :], of.rearrange("(o d) -> o d", o=1).to_broadcast([P, D]))
            for k, of in enumerate((att_src, att_dst)):
                load(att_row[:, k, :], of.rearrange("(o h) d -> o (h d)", o=1).to_broadcast([P, D]))
            with nc.allow_non_contiguous_dma(reason="three vectors of 256, feature by partition"):
                for to, of in ((g_col, ln_g), (b_col, ln_b), (m1_col, bm1)):
                    load(to[:, :], of.rearrange("(t p) -> p t", p=P))

        def weights_vec(dve):
            v = nc.vector
            dve.wait_ge(weights_in, 16 * N_WEIGHTS)
            n_line = [0]

            def line(ins):
                n_line[0] += 1
                ins.then_inc(weights_dve, 1)
                dve.wait_ge(weights_dve, n_line[0])
            for k in range(2):
                line(v.tensor_tensor(att_mul[:, :, :], w_gat[:, :, :],
                                     att_row[:, k, :].unsqueeze(1).to_broadcast([P, 2, D]), ALU.mult))
                line(v.tensor_reduce(w_att[:, :, k * HEADS:(k + 1) * HEADS],
                                     att_mul[:, :, :].rearrange("p t (h d) -> p t h d", d=HD), AXX, ALU.add))
            for t in range(2):
                line(v.tensor_scalar(w_m1[:, t, :], w_m1_in[:, t, :], g_col[:, t:t + 1], None, ALU.mult))
            dve.wait_ge(weights_pe, 1)
            for t in range(2):
                line(v.tensor_copy(w0t[:, t, :], bank[t][:, 0:D]))
            line(v.tensor_tensor(m1_col[:, :], m1_col[:, :], bank[2][:, 0:2], ALU.add))

        def weights_tensor(pe):
            m = nc.tensor
            pe.wait_ge(weights_in, 16 * N_WEIGHTS)
            pe.wait_ge(same_made[0].sem, same_made[0].at(NC // 4 - 1))
            for kt in range(2):
                for nt in range(2):
                    m.transpose(bank[kt][:, nt * P:(nt + 1) * P], w0_in[:, nt, kt * P:(kt + 1) * P], ident[:, :])
            for f in range(2):
                for t in range(2):
                    last = m.matmul(bank[2][:, f:f + 1], w_m1_in[:, t, f * P:(f + 1) * P], b_col[:, t:t + 1],
                                    start=t == 0, stop=t == 1)
            last.then_inc(weights_pe, 1)

        tmp.close()

        got = sb("got", [P, U, XW])
        done = sb("done", [P, U, XW])
        near = sb("near", [P, U, P])
        from_at = sb("from_at", [P, U, 2], I32)
        to_at = sb("to_at", [P, U], I32)
        d_got = sb("d_got", [P, U, 1])
        d_edge = sb("d_edge", [P, U, 1])
        RUNS = 5
        tables_done = sem("tables_done")
        from_made = Count(sem("from_made"), 1, NC)
        to_made = Count(sem("to_made"), 1, NC)
        near_made = Count(sem("near_made"), 1, NC)
        d_ready = Count(sem("d_ready"), 1, NC)
        scaled = Count(sem("scaled"), 1, NC)
        carried = Count(sem("carried"), 1, NC)
        summed = Count(sem("summed"), 1, NC)
        copied = Count(sem("copied"), 1, NC)
        gathered = [sem(f"gathered{s}") for s in range(U)]
        d_gathered = [sem(f"d_gathered{s}") for s in range(U)]
        scattered = [sem(f"scattered{s}") for s in range(U)]

        order_of = (0, 0, 0, 0, 1)
        width_of = (D, D, D, XW, D)
        from_of = (x, y1, x1, xp, x3)
        to_of = (sums, sums, sums, sums_gat, sums_src)

        def landed(run, t):
            return 16 * (run * (NC // U) + 1) + t * 16

        def edges_pool(pool, run):
            o, w = order_of[run], width_of[run]

            def gather(c, s, t):
                pool.wait_ge(from_made.sem, from_made.at(c, run=run))
                if started(c):
                    pool.wait_ge(summed.sem, summed.at(c - U, run=run))
                pool.sem_inc(held, 1)
                nc.gpsimd.indirect_dma_start(
                    got[:, s, 0:D], None, from_of[run],
                    bass.IndirectOffsetOnAxis(ap=from_at[:, s, 0:1], axis=0),
                    bounds_check=N - 1, oob_is_err=False).then_inc(gathered[s], 16)
                if run == 0:
                    nc.gpsimd.indirect_dma_start(
                        d_got[:, s, :], None, dinv_tab,
                        bass.IndirectOffsetOnAxis(ap=from_at[:, s, 0:1], axis=0),
                        bounds_check=N - 1, oob_is_err=False).then_inc(d_gathered[s], 16)

            def scatter(c, s, t):
                pool.wait_ge(to_made.sem, to_made.at(c, run=run))
                pool.wait_ge(copied.sem, copied.at(c, run=run))
                pool.sem_inc(held, 1)
                nc.gpsimd.indirect_dma_start(
                    to_of[run], bass.IndirectOffsetOnAxis(ap=to_at[:, s:s + 1], axis=0),
                    done[:, s, 0:w], None, bounds_check=N - 1, oob_is_err=False).then_inc(scattered[s], 16)

            pool.wait_ge(tables_done, run + 1)
            rounds(pool, NC, [(0, gather), (4, scatter)])

        def edges_dve(dve, run):
            v = nc.vector
            o, w = order_of[run], width_of[run]

            def columns(c, s, t):
                if started(c) or run:
                    dve.wait_ge(gathered[s], landed(run, t) - 16)
                    if run == 0:
                        dve.wait_ge(d_gathered[s], landed(run, t) - 16)
                dve.sem_inc(held, 1)
                v.tensor_copy(from_at[:, s, 0:1], at[o][:, bass.ds(c, 1), 0]).then_inc(from_made.sem, 1)

            def weigh(c, s, t):
                if run == 0:
                    dve.wait_ge(d_gathered[s], landed(run, t))
                    v.tensor_scalar(d_edge[:, s, :], d_got[:, s, :], not0[:, 0:1], is0[:, 0:1],
                                    ALU.mult, ALU.add).then_inc(d_ready.sem, 1)
                    dve.wait_ge(d_ready.sem, d_ready.at(c))
                if started(c):
                    dve.wait_ge(summed.sem, summed.at(c - U, run=run))
                by = (d_edge[:, s, :] if run == 0 else weight[:, bass.ds(c, 1)] if run == 4 else 1.0)
                v.tensor_scalar(near[:, s, :], same[:, bass.ds(c, 1), :].rearrange("p c m -> p (c m)"),
                                by, None, ALU.mult).then_inc(near_made.sem, 1)
                if run == 3:
                    dve.wait_ge(gathered[s], landed(run, t))
                    v.tensor_tensor(got[:, s, 0:D].rearrange("p (h d) -> p h d", d=HD),
                                    got[:, s, 0:D].rearrange("p (h d) -> p h d", d=HD),
                                    p_and_m[:, bass.ds(c, 1), 0:HEADS].rearrange("p c h -> p (c h)")
                                    .unsqueeze(2).to_broadcast([P, HEADS, HD]), ALU.mult)
                    v.tensor_scalar(got[:, s, D:XW], p_and_m[:, bass.ds(c, 1), :].rearrange("p c h -> p (c h)"),
                                    1.0, None, ALU.mult).then_inc(scaled.sem, 1)

            def targets(c, s, t):
                if started(c) or run:
                    dve.wait_ge(scattered[s], landed(run, t) - 16)
                dve.sem_inc(held, 1)
                v.tensor_copy(to_at[:, s:s + 1], at[o][:, bass.ds(c, 1), 1]).then_inc(to_made.sem, 1)

            rounds(dve, NC, [(0, columns), (2, weigh), (3, targets)])

        def edges_pe(pe, run):
            w = width_of[run]

            def add(c, s, t):
                pe.wait_ge(near_made.sem, near_made.at(c, run=run))
                pe.wait_ge(carried.sem, carried.at(c, run=run))
                if started(c, 2):
                    pe.wait_ge(copied.sem, copied.at(c - 2, run=run))
                nc.tensor.matmul(bank[s % 2][:, 0:w], near[:, s, :], got[:, s, 0:w],
                                 start=True, stop=True).then_inc(summed.sem, 1)
            rounds(pe, NC, [(2, add)])

        def edges_act(act, run):
            w = width_of[run]

            def carry(c, s, t):
                if run == 3:
                    act.wait_ge(scaled.sem, scaled.at(c))
                act.wait_ge(gathered[s], landed(run, t))
                if isinstance(c, int) and c == 0:
                    nc.scalar.activation(got[0:1, s, 0:w], zero_w[0:1, 0:w], ACT.Copy).then_inc(carried.sem, 1)
                    return
                act.wait_ge(summed.sem, summed.at(c - 1, run=run))
                nc.scalar.activation(got[0:1, s, 0:w], bank[(s - 1) % 2][0:1, 0:w],
                                     ACT.Copy).then_inc(carried.sem, 1)

            def collect(c, s, t):
                act.wait_ge(summed.sem, summed.at(c, run=run))
                if started(c) or run:
                    act.wait_ge(scattered[s], landed(run, t) - 16)
                nc.scalar.activation(done[:, s, 0:w], bank[s % 2][:, 0:w], ACT.Copy).then_inc(copied.sem, 1)
            rounds(act, NC, [(2, carry), (3, collect)])

        zero_w_made = sem("zero_w_made")

        ends = sb("ends", [P, NC, 3 * HEADS])
        p_and_m = sb("p_and_m", [P, NC, 2 * HEADS])
        a_got = sb("a_got", [P, U, 2, 2 * HEADS])
        a_from = sb("a_from", [P, U, 2], I32)
        a_gathered = [sem(f"a_gathered{s}") for s in range(U)]
        a_from_made = Count(sem("a_from_made"), 1, NC)
        a_kept = Count(sem("a_kept"), 1, NC)
        piece = sb("piece", [P, 2, 4, HEADS])
        piece_gate = sb("piece_gate", [P, 2, 4, HEADS], BF16)
        turn = sb("turn", [P, 2, 4 * HEADS])
        NQ = NC // 4
        piece_made = Count(sem("piece_made"), 1, NQ)
        heads_up = Count(sem("heads_up"), 1, NQ)
        gates_in = Count(sem("gates_in"), 1, NQ)
        scanned = Count(sem("scanned"), 1, NQ)
        edges_up = Count(sem("edges_up"), 1, NQ)
        turned_in = Count(sem("turned_in"), 1, NQ)
        mirrored = Count(sem("mirrored"), 1, NQ)
        max_kept = Count(sem("max_kept"), 1, NQ)
        soft_dve = sem("soft_dve")
        soft_act = sem("soft_act")

        def attention_pool(pool):
            def gather(c, s, t):
                pool.wait_ge(a_from_made.sem, a_from_made.at(c))
                if started(c):
                    pool.wait_ge(a_kept.sem, a_kept.at(c - U))
                pool.sem_inc(held, 1)
                for k in range(2):
                    nc.gpsimd.indirect_dma_start(
                        a_got[:, s, k, :], None, a16,
                        bass.IndirectOffsetOnAxis(ap=a_from[:, s, k:k + 1], axis=0),
                        bounds_check=N - 1, oob_is_err=False).then_inc(a_gathered[s], 16)
            pool.wait_ge(tables_done, 4)
            rounds(pool, NC, [(0, gather)])

        def attention_dve(dve):
            v = nc.vector

            def columns(c, s, t):
                if started(c):
                    dve.wait_ge(a_gathered[s], 32 * t)
                dve.sem_inc(held, 1)
                v.tensor_copy(a_from[:, s, :], at[0][:, bass.ds(c, 1), 0:3:2].rearrange("p c k -> p (c k)")
                              ).then_inc(a_from_made.sem, 1)

            def keep(c, s, t):
                dve.wait_ge(a_gathered[s], 32 * t + 32)
                v.tensor_scalar(ends[:, bass.ds(c, 1), 0:HEADS].rearrange("p c h -> p (c h)"),
                                a_got[:, s, 0, 0:HEADS], not0[:, 0:1], neg0[:, 0:1], ALU.mult, ALU.add)
                v.tensor_scalar(ends[:, bass.ds(c, 1), HEADS:].rearrange("p c h -> p (c h)"),
                                a_got[:, s, 1, :], 1.0, None, ALU.mult).then_inc(a_kept.sem, 1)

            def arrive(new, old):
                for c in range(4):
                    if new:
                        columns(new[0] * 4 + c, c, new[0])
                    if old:
                        keep(old[0] * 4 + c, c, old[0])

            for back in range(2):
                source = run_max if back else ends
                gate = gate_bwd if back else gate_fwd

                def chunk(q, back=back):
                    return (NC - 4 - q * 4) if back else q * 4

                def lay(q, s, t, back=back, source=source, gate=gate, chunk=chunk):
                    if started(q, 2):
                        dve.wait_ge(heads_up.sem, heads_up.at(q - 2, run=back))
                    if not back:
                        dve.wait_ge(a_kept.sem, a_kept.at(q * 4 + 3))
                    v.tensor_scalar(piece[:, s, :, :], source[:, bass.ds(chunk(q), 4), 0:HEADS],
                                    1.0, None, ALU.mult)
                    v.tensor_scalar(piece_gate[:, s, :, :], gate[:, bass.ds(chunk(q), 4)].unsqueeze(2)
                                    .to_broadcast([P, 4, HEADS]), 1.0, None, ALU.mult
                                    ).then_inc(piece_made.sem, 1)

                def climb(q, s, t, back=back):
                    dve.wait_ge(gates_in.sem, gates_in.at(q, run=back))
                    if started(q, 1):
                        dve.wait_ge(scanned.sem, scanned.at(q - 1, run=back))
                    if started(q, 2):
                        dve.wait_ge(edges_up.sem, edges_up.at(q - 2, run=back))
                    start = -BIG if isinstance(q, int) and q == 0 else scan[:, 1 - s, 4 * P - 1:4 * P]
                    v.tensor_tensor_scan(scan[:, s, :], gates[:, s, :], bank[2 + s][0:HEADS, :], start,
                                         ALU.add, ALU.max).then_inc(scanned.sem, 1)

                def keep_max(q, s, t, back=back, chunk=chunk):
                    if back:
                        dve.wait_ge(mirrored.sem, mirrored.at(q))
                        v.tensor_scalar(p_and_m[:, bass.ds(chunk(q), 4), HEADS:],
                                        bank[6 + s][:, 64:96].rearrange("p (c h) -> p c h", h=HEADS),
                                        1.0, None, ALU.mult).then_inc(max_kept.sem, 1)
                    else:
                        dve.wait_ge(edges_up.sem, edges_up.at(q))
                        v.tensor_scalar(run_max[:, bass.ds(chunk(q), 4), :],
                                        bank[6 + s][:, 0:32].rearrange("p (c h) -> p c h", h=HEADS),
                                        not0[:, 0:1], neg0[:, 0:1], ALU.mult, ALU.add).then_inc(max_kept.sem, 1)
                rounds(dve, NQ, [(5, keep_max), (2, climb), (0, lay)] if back else
                       [((0, 1), arrive), (6, keep_max), (4, climb), (2, lay)], 2)
                dve.wait_ge(max_kept.sem, max_kept.at(NQ - 1, run=back))

            n_line = [0]

            def line(ins):
                n_line[0] += 1
                ins.then_inc(soft_dve, 1)
                dve.wait_ge(soft_dve, n_line[0])
            own, self_s, self_d = (ends[:, :, k * HEADS:(k + 1) * HEADS] for k in range(3))
            weights, top = p_and_m[:, :, 0:HEADS], p_and_m[:, :, HEADS:]
            line(v.tensor_tensor(top, top, self_s, ALU.max))
            line(v.tensor_tensor(top, top, self_d, ALU.add))
            line(v.scalar_tensor_tensor(top, top, 0.2, top, ALU.mult, ALU.max))
            line(v.tensor_tensor(own, own, self_d, ALU.add))
            line(v.scalar_tensor_tensor(own, own, 0.2, own, ALU.mult, ALU.max))
            line(v.tensor_tensor(weights, own, top, ALU.subtract))
            line(v.tensor_tensor(top, top, first[:, :].unsqueeze(2).to_broadcast([P, NC, HEADS]), ALU.mult))
            dve.wait_ge(soft_act, 1)

        def attention_pe(pe):
            m = nc.tensor
            for back in range(2):
                by, by_b = (flip, flip_b) if back else (ident, ident_b)

                def up_(q, s, t, back=back, by=by, by_b=by_b):
                    pe.wait_ge(piece_made.sem, piece_made.at(q, run=back))
                    if started(q, 2):
                        pe.wait_ge(scanned.sem, scanned.at(q - 2, run=back))
                        pe.wait_ge(gates_in.sem, gates_in.at(q - 2, run=back))
                    for b, of, turn_by in ((2, piece, by), (4, piece_gate, by_b)):
                        for c in range(4):
                            last = m.matmul(bank[b + s][0:HEADS, c * P:(c + 1) * P],
                                            of[:, s, 3 - c if back else c, :], turn_by[:, :],
                                            start=True, stop=True)
                    last.then_inc(heads_up.sem, 1)

                def down_(q, s, t, back=back):
                    pe.wait_ge(scanned.sem, scanned.at(q, run=back))
                    if started(q, 2):
                        pe.wait_ge(max_kept.sem, max_kept.at(q - 2, run=back))
                    for c in range(4):
                        at_c = (3 - c if back else c) * HEADS
                        last = m.matmul(bank[6 + s][:, at_c:at_c + HEADS], scan[:, s, c * P:(c + 1) * P],
                                        ident[0:HEADS, 0:HEADS], start=True, stop=True)
                    last.then_inc(edges_up.sem, 1)

                def mirror(q, s, t):
                    pe.wait_ge(turned_in.sem, turned_in.at(q))
                    m.matmul(bank[6 + s][:, 64:96], flip[:, :], turn[:, s, :],
                             start=True, stop=True).then_inc(mirrored.sem, 1)
                rounds(pe, NQ, ([(4, mirror)] if back else []) + [(3, down_), (0, up_)], 2)

        def attention_act(act):
            for back in range(2):
                def gates_copy(q, s, t, back=back):
                    act.wait_ge(heads_up.sem, heads_up.at(q, run=back))
                    if started(q, 2):
                        act.wait_ge(scanned.sem, scanned.at(q - 2, run=back))
                    nc.scalar.activation(gates[:, s, :], bank[4 + s][0:HEADS, :],
                                         ACT.Copy).then_inc(gates_in.sem, 1)

                def turn_copy(q, s, t):
                    act.wait_ge(edges_up.sem, edges_up.at(q, run=1))
                    if started(q, 2):
                        act.wait_ge(mirrored.sem, mirrored.at(q - 2))
                    nc.scalar.activation(turn[:, s, :], bank[6 + s][:, 0:32], ACT.Copy
                                         ).then_inc(turned_in.sem, 1)
                rounds(act, NQ, ([(3, turn_copy)] if back else []) + [(0, gates_copy)], 2)
            act.wait_ge(soft_dve, 6)
            weights = p_and_m[:, :, 0:HEADS]
            nc.scalar.activation(weights, weights, ACT.Exp).then_inc(soft_act, 1)

        RA = 2 * U
        ring_a = sb("ring_a", [P, RA, J, D])
        ring_s = sb("ring_s", [P, U, J, XW])
        ring_b = sb("ring_b", [P, U, J, D])
        ring_o = sb("ring_o", [P, U, J, D])
        ring_z = sb("ring_z", [P, U, J, D])
        mix = sb("mix", [P, 2, J, D])
        feat = [sb(f"feat{k}", [P, 2, 2, J * P]) for k in range(2)]
        hid = sb("hid", [P, 2, 2, J * P])
        run_max = ring_a[:, :, :, :].rearrange("p s j d -> p (s j d)")[:, 0:NC * HEADS] \
            .rearrange("p (c h) -> p c h", h=HEADS)
        gates = ring_z[0:HEADS, :, :, :].rearrange("p s j d -> p s (j d)")
        scan = mix[0:HEADS, :, :, :].rearrange("p s j d -> p s (j d)")
        junk = sb("junk", [P, J, D], BF16)
        scores = sb("scores", [P, U, J, 2 * HEADS])
        small = sb("small", [P, U, 6, J * HEADS])
        stat = sb("stat", [P, 2, U, J, 6])
        mv = sb("mv", [P, 2, U, J, 2])
        norm = sb("norm", [P, 2, 4, U, J])
        soft = sb("soft", [P, 3, U, J])

        loads_of = (2, 2, 2, 2, 2)
        loaded = [sem(f"loaded{s}") for s in range(U)]
        loaded_late = [sem(f"loaded_late{s}") for s in range(U)]
        stored_proj = [sem(f"stored_proj{s}") for s in range(U)]
        stored = [sem(f"stored{s}") for s in range(U)]
        NT = NG // U

        def loads(step, t):
            return 16 * sum(loads_of[:step]) * NT + 16 * loads_of[step] * (t + 1)

        def stores(step, t):
            return 16 * step * NT + 16 * (t + 1)

        def loads_late(step, t):
            return 16 * (t + 1) if step == 1 else 16 * NT + 32 * (t + 1)

        def group(table, g):
            return table[bass.ds(g * GROUP, GROUP), :].rearrange("(p j) d -> p j d", j=J)

        def flat(ap):
            return ap.rearrange("p j d -> p (j d)")

        def fetch(sp, table, g, buf, slot, signal, w=D):
            if table is x and isinstance(g, int) and g == NG - 1:
                sp.dma_start(buf[0:LAST, slot, :, 0:w],
                             table[g * GROUP:N, :].rearrange("(p j) d -> p j d", j=J)
                             ).then_inc(signal, 16)
            else:
                sp.dma_start(buf[:, slot, :, 0:w], group(table, g)).then_inc(signal, 16)

        def put_out(sp, table, g, buf, slot, signal):
            if table is out and isinstance(g, int) and g == NG - 1:
                sp.dma_start(table[g * GROUP:N, :].rearrange("(p j) d -> p j d", j=J),
                             buf[0:LAST, slot, :, :]).then_inc(signal, 16)
            else:
                sp.dma_start(group(table, g), buf[:, slot, :, :]).then_inc(signal, 16)

        def sums_complete(sp, step):
            for s in range(U):
                sp.wait_ge(scattered[s], landed(step, NC // U - 1))

        def step_complete(sp, step):
            for s in range(U):
                sp.wait_ge(stored[s], stores(step, NT - 1))
            sp.sem_inc(tables_done, 1)

        def norm_counts(name, k=0):
            return Count(sem(name + "_stats"), 4), Count(sem(name + "_roots"), 2), Count(sem(name + "_fixed"), 4), k

        def norm_stats(dve, counts, g, s, z, k):
            v = nc.vector
            stats, roots, fixed, b = counts
            if k == 0:
                v.bn_stats(stat[:, b, s, 0, :], z[:, 0, :]).then_inc(stats.sem, 1)
                last = v.bn_stats(stat[:, b, s, 1, :], z[:, 1, :])
            elif k == 1:
                dve.wait_ge(stats.sem, stats.at(g, 2))
                dve.sem_inc(held, 1)
                for j in range(J):
                    last = v.bn_aggr(mv[:, b, s, j, :], stat[:, b, s, j, :])
            else:
                dve.wait_ge(stats.sem, stats.at(g, 3))
                last = v.tensor_scalar(norm[:, b, 0, s, :], mv[:, b, s, :, 1], 1e-5, None, ALU.add)
            last.then_inc(stats.sem, 1)

        def norm_roots(act, counts, g, s):
            stats, roots, fixed, k = counts
            act.wait_ge(stats.sem, stats.at(g))
            nc.scalar.activation(norm[:, k, 1, s, :], norm[:, k, 0, s, :], ACT.Ln).then_inc(roots.sem, 1)
            act.wait_ge(roots.sem, roots.at(g, 1))
            nc.scalar.activation(norm[:, k, 1, s, :], norm[:, k, 1, s, :], ACT.Exp,
                                 scale=-0.5).then_inc(roots.sem, 1)

        def norm_refine(dve, counts, g, s, k):
            v = nc.vector
            stats, roots, fixed, b = counts
            var, y, w, off = (norm[:, b, q, s, :] for q in range(4))
            if k == 0:
                dve.wait_ge(roots.sem, roots.at(g))
                last = v.scalar_tensor_tensor(w, y, -0.5, y, ALU.mult, ALU.mult)
            elif k == 1:
                dve.wait_ge(fixed.sem, fixed.at(g, 1))
                last = v.tensor_tensor(w, w, var, ALU.mult)
            elif k == 2:
                dve.wait_ge(fixed.sem, fixed.at(g, 2))
                last = v.scalar_tensor_tensor(y, w, 1.5, y, ALU.add, ALU.mult)
            else:
                dve.wait_ge(fixed.sem, fixed.at(g, 3))
                last = v.scalar_tensor_tensor(off, mv[:, b, s, :, 0], -1.0, y, ALU.mult, ALU.mult)
            last.then_inc(fixed.sem, 1)

        def norm_apply(act, counts, g, s, to, z, signal):
            stats, roots, fixed, k = counts
            act.wait_ge(fixed.sem, fixed.at(g))
            for j in range(J):
                last = nc.scalar.activation(to[:, j, :], z[:, j, :], ACT.Identity,
                                            bias=norm[:, k, 3, s, j:j + 1], scale=norm[:, k, 1, s, j:j + 1])
            last.then_inc(signal.sem, 1)

        def turn_rows(of, to):
            for h in range(2):
                for j in range(J):
                    last = nc.tensor.transpose(to[:, (h * J + j) * P:(h * J + j + 1) * P],
                                               of[:, j, h * P:(h + 1) * P], ident[:, :])
            return last

        def times(to, terms, w=D, at_=0):
            for j in range(J):
                n = 0
                for f, wt in terms:
                    for h in range(2):
                        last = nc.tensor.matmul(to[:, at_ + j * w:at_ + (j + 1) * w], f[:, h, j * P:(j + 1) * P],
                                                wt[:, h, :], start=n == 0, stop=n == 2 * len(terms) - 1)
                        n += 1
            return last

        def row2(r):
            return r[:, :].unsqueeze(1).to_broadcast([P, J, D])

        def psum2(b):
            return bank[b][:, :].rearrange("p (j d) -> p j d", j=J)

        a_sum = Count(sem("a_sum"))
        a_out = Count(sem("a_out"))

        def hop_sync(sp):
            def load(g, s, t):
                if started(g):
                    sp.wait_ge(a_sum.sem, a_sum.at(g - U))
                    sp.sem_inc(held, 1)
                fetch(sp, x, g, ring_a, s, loaded[s])
                fetch(sp, sums, g, ring_s, s, loaded[s])

            def store(g, s, t):
                sp.wait_ge(a_out.sem, a_out.at(g))
                sp.sem_inc(held, 1)
                put_out(sp, y1, g, ring_o, s, stored[s])

            sums_complete(sp, 0)
            rounds(sp, NG, [(0, load), (5, store)], U, peel=True)
            step_complete(sp, 0)

        def hop_dve(dve):
            def add(g, s, t):
                dve.wait_ge(loaded[s], loads(0, t))
                if started(g, 2):
                    dve.wait_ge(a_out.sem, a_out.at(g - 2))
                for j in range(J):
                    last = nc.vector.scalar_tensor_tensor(
                        ring_z[:, s, j, :], ring_a[:, s, j, :],
                        dinv[:, bass.ds(g, 1), j], ring_s[:, s, j, 0:D], ALU.mult, ALU.add)
                last.then_inc(a_sum.sem, 1)
            rounds(dve, NG, [(0, add)])

        def hop_act(act):
            def scale(g, s, t):
                act.wait_ge(a_sum.sem, a_sum.at(g))
                if started(g):
                    act.wait_ge(stored[s], stores(0, t - 1))
                act.sem_inc(held, 1)
                for j in range(J):
                    last = nc.scalar.activation(ring_o[:, s, j, :], ring_z[:, s, j, :], ACT.Copy,
                                                scale=dinv2[:, bass.ds(g, 1), j])
                last.then_inc(a_out.sem, 1)
            rounds(act, NG, [(0, scale)])

        b_sum = Count(sem("b_sum"))
        b_up = Count(sem("b_up"))
        b_feat = Count(sem("b_feat"))
        b_logit = Count(sem("b_logit"))
        b_max = Count(sem("b_max"), 2)
        b_exp = Count(sem("b_exp"), 2)
        b_res = Count(sem("b_res"), 2)
        b_out = Count(sem("b_out"))
        b_norm = norm_counts("b_norm")
        logit = ring_b

        def sgc_sync(sp):
            def load(g, s, t):
                if started(g):
                    sp.wait_ge(b_sum.sem, b_sum.at(g - U))
                    sp.sem_inc(held, 1)
                fetch(sp, y1, g, ring_a, s, loaded[s])
                fetch(sp, sums, g, ring_s, s, loaded[s])

            def load_x(g, s, t):
                if started(g):
                    sp.wait_ge(b_res.sem, b_res.at(g - U))
                    sp.sem_inc(held, 1)
                fetch(sp, x, g, ring_a, U + s, loaded_late[s])

            def store(g, s, t):
                sp.wait_ge(b_out.sem, b_out.at(g))
                sp.sem_inc(held, 1)
                put_out(sp, x1, g, ring_o, s, stored[s])

            sums_complete(sp, 1)
            rounds(sp, NG, [(0, load), (3, load_x), (10, store)], U, peel=True)
            step_complete(sp, 1)

        def sgc_pool(pool):
            def add(g, s, t):
                pool.wait_ge(loaded[s], loads(1, t))
                if started(g, 2):
                    pool.wait_ge(b_up.sem, b_up.at(g - 2))
                nc.gpsimd.tensor_tensor(mix[:, s % 2, :, :], ring_a[:, s, :, :], ring_s[:, s, :, 0:D], ALU.add
                                        ).then_inc(b_sum.sem, 1)
            rounds(pool, NG, [(0, add)])

        def sgc_dve(dve):
            v = nc.vector

            def bias(g, s, t, k):
                if k == 0:
                    dve.wait_ge(b_logit.sem, b_logit.at(g))
                    if started(g):
                        dve.wait_ge(b_res.sem, b_res.at(g - U))
                    for j in range(J):
                        last = v.scalar_tensor_tensor(logit[:, s, j, :], psum2(4 + s % 2)[:, j, :],
                                                      dinv[:, bass.ds(g, 1), j], b0_row[:, :], ALU.mult, ALU.add)
                else:
                    dve.wait_ge(b_max.sem, b_max.at(g, 1))
                    last = v.tensor_reduce(soft[:, 0, s, :], logit[:, s, :, :], AXX, ALU.max, negate=True)
                last.then_inc(b_max.sem, 1)

            def residual(g, s, t, k):
                if k == 0:
                    dve.wait_ge(b_exp.sem, b_exp.at(g))
                    v.tensor_tensor(soft[:, 0, s, :], soft[:, 0, s, :], soft[:, 2, s, :], ALU.subtract
                                    ).then_inc(b_res.sem, 1)
                elif k == 1:
                    dve.wait_ge(loaded_late[s], loads_late(1, t))
                    dve.wait_ge(b_res.sem, b_res.at(g, 1))
                    if started(g):
                        dve.wait_ge(b_out.sem, b_out.at(g - U))
                    for j in range(J):
                        last = v.scalar_tensor_tensor(ring_z[:, s, j, :], logit[:, s, j, :],
                                                      soft[:, 0, s, j:j + 1], ring_a[:, U + s, j, :],
                                                      ALU.add, ALU.add)
                    last.then_inc(b_res.sem, 1)
                else:
                    if k == 2:
                        dve.wait_ge(b_res.sem, b_res.at(g, 2))
                    norm_stats(dve, b_norm, g, s, ring_z[:, s, :, :], k - 2)

            def all_stages(fix, res, top):
                for k in range(5):
                    if fix and k < 4:
                        norm_refine(dve, b_norm, *fix[:2], k)
                    if res:
                        residual(*res, k)
                    if top and k in (1, 3):
                        bias(*top, k // 2)
            rounds(dve, NG, [((6, 4, 2), all_stages)])

        def sgc_pe(pe):
            def up_(g, s, t):
                pe.wait_ge(b_sum.sem, b_sum.at(g))
                if started(g, 2):
                    pe.wait_ge(b_feat.sem, b_feat.at(g - 2))
                turn_rows(mix[:, s % 2, :, :], bank[2 + s % 2]).then_inc(b_up.sem, 1)

            def mul(g, s, t):
                pe.wait_ge(b_feat.sem, b_feat.at(g))
                if started(g, 2):
                    pe.wait_ge(b_max.sem, b_max.at(g - 2, 1))
                times(bank[4 + s % 2], [(feat[0][:, s % 2, :, :], w0t)]).then_inc(b_logit.sem, 1)
            rounds(pe, NG, [(0, up_), (1, mul)])

        def sgc_act(act):
            a = nc.scalar

            def copy(g, s, t):
                act.wait_ge(b_up.sem, b_up.at(g))
                if started(g, 2):
                    act.wait_ge(b_logit.sem, b_logit.at(g - 2))
                a.activation(feat[0][:, s % 2, :, :].rearrange("p h n -> p (h n)"), bank[2 + s % 2][:, :],
                             ACT.Copy).then_inc(b_feat.sem, 1)

            def expo(g, s, t):
                act.wait_ge(b_max.sem, b_max.at(g))
                if started(g, 1):
                    act.wait_ge(b_exp.sem, b_exp.at(g - 1))
                for j in range(J):
                    last = a.activation(junk[:, j, :], logit[:, s, j, :], ACT.Exp, bias=soft[:, 0, s, j:j + 1],
                                        accum_out=soft[:, 1, s, j:j + 1])
                last.then_inc(b_exp.sem, 1)
                act.wait_ge(b_exp.sem, b_exp.at(g, 1))
                a.activation(soft[:, 2, s, :], soft[:, 1, s, :], ACT.Ln).then_inc(b_exp.sem, 1)

            def result(g, s, t):
                if started(g):
                    act.wait_ge(stored[s], stores(1, t - 1))
                norm_apply(act, b_norm, g, s, ring_o[:, s, :, :], ring_z[:, s, :, :], b_out)
            def roots(g, s, t):
                norm_roots(act, b_norm, g, s)
            rounds(act, NG, [(6, result), (4, roots), (2, expo), (0, copy)])

        c_mean = Count(sem("c_mean"))
        c_up = Count(sem("c_up"), 2)
        c_feat = Count(sem("c_feat"), 2)
        c_mul = Count(sem("c_mul"))
        c_res = Count(sem("c_res"), 2)
        c_out = Count(sem("c_out"))
        c_up2 = Count(sem("c_up2"))
        c_feat2 = Count(sem("c_feat2"))
        c_proj = Count(sem("c_proj"))
        c_xp = Count(sem("c_xp"))
        c_sc = Count(sem("c_sc"))
        c_norm = norm_counts("c_norm")
        MUL, PROJ = (4, 0), (6, 1)

        def sage_sync(sp):
            def load(g, s, t):
                if started(g):
                    sp.wait_ge(c_res.sem, c_res.at(g - U))
                    sp.sem_inc(held, 1)
                    sp.wait_ge(c_up.sem, c_up.at(g - U))
                    sp.sem_inc(held, 1)
                    sp.wait_ge(c_mean.sem, c_mean.at(g - U))
                    sp.sem_inc(held, 1)
                fetch(sp, x1, g, ring_a, s, loaded[s])
                fetch(sp, sums, g, ring_s, s, loaded[s])

            def store(g, s, t):
                sp.wait_ge(c_out.sem, c_out.at(g))
                sp.sem_inc(held, 1)
                put_out(sp, x2, g, ring_o, s, stored[s])

            def store_proj(g, s, t):
                sp.wait_ge(c_xp.sem, c_xp.at(g))
                sp.sem_inc(held, 1)
                sp.wait_ge(c_sc.sem, c_sc.at(g))
                sp.sem_inc(held, 1)
                put_out(sp, xp, g, ring_b, s, stored_proj[s])
                put_out(sp, a16, g, scores, s, stored_proj[s])

            sums_complete(sp, 2)
            rounds(sp, NG, [(0, load), (6, store), (9, store_proj)], U, peel=True)
            for s in range(U):
                sp.wait_ge(stored_proj[s], 32 * NT)
            step_complete(sp, 2)

        def sage_dve(dve):
            v = nc.vector

            def mean(g, s, t):
                dve.wait_ge(loaded[s], loads(2, t))
                if started(g, 2):
                    dve.wait_ge(c_up.sem, c_up.at(g - 2))
                for j in range(J):
                    last = v.tensor_scalar(mix[:, s % 2, j, :], ring_s[:, s, j, 0:D], rdeg[:, bass.ds(g, 1), j],
                                           None, ALU.mult)
                last.then_inc(c_mean.sem, 1)

            def residual(g, s, t, k):
                z = ring_z[:, s, :, :]
                if k == 0:
                    dve.wait_ge(c_mul.sem, c_mul.at(g))
                    if started(g, 2):
                        dve.wait_ge(c_out.sem, c_out.at(g - 2))
                    v.tensor_tensor(z, psum2(MUL[s % 2]), row2(b1_row), ALU.add).then_inc(c_res.sem, 1)
                elif k == 1:
                    dve.wait_ge(c_res.sem, c_res.at(g, 1))
                    v.scalar_tensor_tensor(flat(z), flat(z), 0.0, flat(ring_a[:, s, :, :]), ALU.max, ALU.add
                                           ).then_inc(c_res.sem, 1)
                else:
                    if k == 2:
                        dve.wait_ge(c_res.sem, c_res.at(g, 2))
                    norm_stats(dve, c_norm, g, s, z, k - 2)

            def scores_out(g, s, t):
                dve.wait_ge(c_proj.sem, c_proj.at(g))
                if started(g):
                    dve.wait_ge(stored_proj[s], 32 * t)
                v.tensor_copy(scores[:, s, :, :], bank[7][:, 0:4 * HEADS].rearrange("p (j h) -> p j h", j=J)
                              ).then_inc(c_sc.sem, 1)

            def refine_and_residual(fix, res):
                for k in range(5):
                    if fix and k < 4:
                        norm_refine(dve, c_norm, *fix[:2], k)
                    if res:
                        residual(*res, k)
            rounds(dve, NG, [(6, scores_out), ((3, 2), refine_and_residual), (0, mean)])

        def sage_pe(pe):
            def up_(g, s, t):
                pe.wait_ge(loaded[s], loads(2, t))
                if started(g, 1):
                    pe.wait_ge(c_feat.sem, c_feat.at(g - 1))
                turn_rows(ring_a[:, s, :, :], bank[2]).then_inc(c_up.sem, 1)
                pe.wait_ge(c_mean.sem, c_mean.at(g))
                turn_rows(mix[:, s % 2, :, :], bank[3]).then_inc(c_up.sem, 1)

            def mul(g, s, t):
                pe.wait_ge(c_feat.sem, c_feat.at(g))
                if started(g, 2):
                    pe.wait_ge(c_res.sem, c_res.at(g - 2, 1))
                times(bank[MUL[s % 2]], [(feat[0][:, s % 2, :, :], w_self), (feat[1][:, s % 2, :, :], w_neigh)]
                      ).then_inc(c_mul.sem, 1)

            def up2(g, s, t):
                pe.wait_ge(c_out.sem, c_out.at(g))
                if started(g, 1):
                    pe.wait_ge(c_feat2.sem, c_feat2.at(g - 1))
                turn_rows(ring_o[:, s, :, :], bank[5]).then_inc(c_up2.sem, 1)

            def project(g, s, t):
                pe.wait_ge(c_feat2.sem, c_feat2.at(g))
                if started(g, 2):
                    pe.wait_ge(c_xp.sem, c_xp.at(g - 2))
                if started(g, 1):
                    pe.wait_ge(c_sc.sem, c_sc.at(g - 1))
                f = hid[:, s % 2, :, :]
                times(bank[PROJ[s % 2]], [(f, w_gat)])
                times(bank[7], [(f, w_att)], 2 * HEADS).then_inc(c_proj.sem, 1)
            pe.wait_ge(copied.sem, copied.at(NC - 1, run=2))
            rounds(pe, NG, [(5, project), (4, up2), (1, mul), (0, up_)])

        def sage_act(act):
            a = nc.scalar

            def copy(g, s, t):
                for k in range(2):
                    act.wait_ge(c_up.sem, c_up.at(g, k + 1))
                    if started(g, 2) and k == 0:
                        act.wait_ge(c_mul.sem, c_mul.at(g - 2))
                    a.activation(feat[k][:, s % 2, :, :].rearrange("p h n -> p (h n)"), bank[2 + k][:, :],
                                 ACT.Copy).then_inc(c_feat.sem, 1)

            def result(g, s, t):
                if started(g):
                    act.wait_ge(stored[s], stores(2, t - 1))
                norm_apply(act, c_norm, g, s, ring_o[:, s, :, :], ring_z[:, s, :, :], c_out)

            def copy2(g, s, t):
                act.wait_ge(c_up2.sem, c_up2.at(g))
                if started(g, 2):
                    act.wait_ge(c_proj.sem, c_proj.at(g - 2))
                a.activation(hid[:, s % 2, :, :].rearrange("p h n -> p (h n)"), bank[5][:, :],
                             ACT.Copy).then_inc(c_feat2.sem, 1)

            def xp_out(g, s, t):
                act.wait_ge(c_proj.sem, c_proj.at(g))
                if started(g):
                    act.wait_ge(stored_proj[s], 32 * t)
                a.activation(flat(ring_b[:, s, :, :]), bank[PROJ[s % 2]][:, :], ACT.Copy).then_inc(c_xp.sem, 1)

            def roots(g, s, t):
                norm_roots(act, c_norm, g, s)
            rounds(act, NG, [(6, xp_out), (4, copy2), (3, result), (2, roots), (0, copy)])

        d_own = Count(sem("d_own"), 4)
        d_pow = Count(sem("d_pow"))
        d_den = Count(sem("d_den"), 4)
        d_loop = Count(sem("d_loop"), 3)
        d_mix = Count(sem("d_mix"))
        d_plus = Count(sem("d_plus"))
        d_nrm = Count(sem("d_nrm"))
        d_up = Count(sem("d_up"))
        d_feat = Count(sem("d_feat"))
        d_hid = Count(sem("d_hid"))
        d_relu = Count(sem("d_relu"))
        d_mul = Count(sem("d_mul"))
        d_res = Count(sem("d_res"))
        d_out = Count(sem("d_out"))
        d_norm1 = norm_counts("d_norm1", 0)
        d_norm2 = norm_counts("d_norm2", 1)

        def gat_sync(sp):
            def load(g, s, t):
                if started(g):
                    sp.wait_ge(d_den.sem, d_den.at(g - U))
                    sp.sem_inc(held, 1)
                fetch(sp, sums_gat, g, ring_s, s % U, loaded[s % U], XW)
                fetch(sp, a16, g, scores, s % U, loaded[s % U], 2 * HEADS)

            def load_rows(g, s, t):
                if started(g):
                    sp.wait_ge(d_mix.sem, d_mix.at(g - U))
                    sp.sem_inc(held, 1)
                fetch(sp, xp, g, ring_b, s % U, loaded_late[s % U])
                if started(g, RA):
                    sp.wait_ge(d_res.sem, d_res.at(g - RA))
                    sp.sem_inc(held, 1)
                fetch(sp, x2, g, ring_a, s, loaded_late[s % U])

            def store(g, s, t):
                sp.wait_ge(d_out.sem, d_out.at(g))
                sp.sem_inc(held, 1)
                put_out(sp, x3, g, ring_o, s % U, stored[s % U])

            sums_complete(sp, 3)
            rounds(sp, NG, [(0, load), (1, load_rows), (11, store)], RA, peel=True)
            step_complete(sp, 3)

        BY_HEAD = "p j (h d) -> p j h d"

        def round_u(g, s, t):
            return t * 2 + (s // U)

        def gat_dve(dve):
            v = nc.vector

            def own(g, s8, t8, k):
                s, t = s8 % U, round_u(g, s8, t8)
                a_s, a_d = scores[:, s, :, 0:HEADS], scores[:, s, :, HEADS:]
                e = small[:, s, 0, :].rearrange("p (j h) -> p j h", j=J)
                if k == 0:
                    dve.wait_ge(loaded[s], loads(3, t))
                    if started(g):
                        dve.wait_ge(d_den.sem, d_den.at(g - U))
                    last = v.tensor_tensor(e, a_s, a_d, ALU.add)
                elif k == 1:
                    dve.wait_ge(d_own.sem, d_own.at(g, 1))
                    last = v.scalar_tensor_tensor(e, e, 0.2, e, ALU.mult, ALU.max)
                elif k == 2:
                    dve.wait_ge(d_own.sem, d_own.at(g, 2))
                    last = v.tensor_tensor(e, e, ring_s[:, s, :, D + HEADS:XW], ALU.subtract)
                else:
                    dve.wait_ge(d_own.sem, d_own.at(g, 3))
                    last = v.tensor_tensor(e, e, has_in[:, bass.ds(g, 1), :].rearrange("p g j -> p (g j)")
                                           .unsqueeze(2).to_broadcast([P, J, HEADS]), ALU.mult)
                last.then_inc(d_own.sem, 1)

            def attend(g, s8, t8, k):
                s = s8 % U
                e, den, r, own_w = (small[:, s, q, :].rearrange("p (j h) -> p j h", j=J) for q in range(4))
                if k == 0:
                    dve.wait_ge(d_pow.sem, d_pow.at(g))
                    v.scalar_tensor_tensor(den, ring_s[:, s, :, D:D + HEADS], 1e-16, e, ALU.add, ALU.add
                                           ).then_inc(d_den.sem, 1)
                elif k == 1:
                    dve.wait_ge(d_den.sem, d_den.at(g, 1))
                    v.reciprocal(r, den).then_inc(d_den.sem, 1)
                elif k == 2:
                    dve.wait_ge(d_den.sem, d_den.at(g, 2))
                    v.tensor_tensor(own_w, e, r, ALU.mult).then_inc(d_den.sem, 1)
                else:
                    if started(g):
                        dve.wait_ge(d_nrm.sem, d_nrm.at(g - U))
                    v.tensor_tensor(ring_z[:, s, :, :].rearrange(BY_HEAD, d=HD),
                                    ring_s[:, s, :, 0:D].rearrange(BY_HEAD, d=HD),
                                    r.unsqueeze(3).to_broadcast([P, J, HEADS, HD]), ALU.mult
                                    ).then_inc(d_den.sem, 1)

            def combine(g, s8, t8, k):
                s = s8 % U
                z = ring_z[:, s, :, :]
                if k == 0:
                    dve.wait_ge(d_den.sem, d_den.at(g))
                    dve.wait_ge(d_loop.sem, d_loop.at(g))
                    v.tensor_tensor(z, z, ring_b[:, s, :, :], ALU.add).then_inc(d_mix.sem, 1)
                else:
                    if k == 1:
                        dve.wait_ge(d_mix.sem, d_mix.at(g))
                    norm_stats(dve, d_norm1, g, s, z, k - 1)

            def residual(g, s8, t8, k):
                s = s8 % U
                z = mlp_z[:, s % 2, :, :]
                if k == 0:
                    dve.wait_ge(d_mul.sem, d_mul.at(g))
                    dve.wait_ge(d_plus.sem, d_plus.at(g))
                    if started(g, 2):
                        dve.wait_ge(d_out.sem, d_out.at(g - 2))
                    v.tensor_tensor(z, psum2(6 + s % 2), ring_a[:, s8, :, :], ALU.add).then_inc(d_res.sem, 1)
                else:
                    if k == 1:
                        dve.wait_ge(d_res.sem, d_res.at(g))
                    norm_stats(dve, d_norm2, g, s, z, k - 1)

            def big_stages(res, mix1):
                for k in range(4):
                    if res:
                        residual(*res, k)
                    if mix1:
                        combine(*mix1, k)

            def scores_stages(att, first_):
                for k in range(4):
                    if att:
                        attend(*att, k)
                    if first_:
                        own(*first_, k)

            def refine_stages(fix2, fix1):
                for k in range(4):
                    if fix1:
                        norm_refine(dve, d_norm1, fix1[0], fix1[1] % U, k)
                    if fix2:
                        norm_refine(dve, d_norm2, fix2[0], fix2[1] % U, k)
            rounds(dve, NG, [((8, 4), refine_stages), ((7, 3), big_stages), ((1, 0), scores_stages)], RA)

        def gat_pool(pool):
            gp = nc.gpsimd

            def loop_rows(g, s8, t8):
                s, t = s8 % U, round_u(g, s8, t8)
                pool.wait_ge(d_den.sem, d_den.at(g, 3))
                pool.wait_ge(loaded_late[s], loads_late(3, t))
                own_w = small[:, s, 3, :].rearrange("p (j h) -> p j h", j=J)
                rows_b = ring_b[:, s, :, :]
                xp_v = rows_b.rearrange(BY_HEAD, d=HD)
                gp.tensor_tensor(xp_v, xp_v, own_w.unsqueeze(3).to_broadcast([P, J, HEADS, HD]), ALU.mult
                                 ).then_inc(d_loop.sem, 1)
                pool.wait_ge(d_loop.sem, d_loop.at(g, 1))
                gp.tensor_tensor(rows_b, rows_b, row2(gat_row), ALU.add).then_inc(d_loop.sem, 1)
                pool.wait_ge(d_loop.sem, d_loop.at(g, 2))
                gp.tensor_tensor(rows_b, rows_b, ring_a[:, s8, :, :], ALU.add).then_inc(d_loop.sem, 1)
                pool.wait_ge(d_loop.sem, d_loop.at(g, 3))
                gp.tensor_tensor(ring_a[:, s8, :, :], ring_a[:, s8, :, :], row2(m2_row), ALU.add
                                 ).then_inc(d_plus.sem, 1)
            rounds(pool, NG, [(1, loop_rows)], RA)

        def gat_pe(pe):
            def up_(g, s, t):
                pe.wait_ge(d_nrm.sem, d_nrm.at(g))
                if started(g, 2):
                    pe.wait_ge(d_feat.sem, d_feat.at(g - 2))
                turn_rows(mix[:, s % 2, :, :], bank[2 + s % 2]).then_inc(d_up.sem, 1)

            def hidden(g, s, t):
                pe.wait_ge(d_feat.sem, d_feat.at(g))
                if started(g, 2):
                    pe.wait_ge(d_relu.sem, d_relu.at(g - 2))
                for f in range(2):
                    for h in range(2):
                        last = nc.tensor.matmul(bank[4 + s % 2][:, f * D:(f + 1) * D],
                                                w_m1[:, h, f * P:(f + 1) * P], feat[0][:, s % 2, h, :],
                                                start=h == 0, stop=h == 1)
                last.then_inc(d_hid.sem, 1)

            def mul(g, s, t):
                pe.wait_ge(d_relu.sem, d_relu.at(g))
                if started(g, 2):
                    pe.wait_ge(d_res.sem, d_res.at(g - 2))
                times(bank[6 + s % 2], [(hid[:, s % 2, :, :], w_m2)]).then_inc(d_mul.sem, 1)
            rounds(pe, NG, [(6, mul), (5, hidden), (4, up_)], RA)

        def gat_act(act):
            a = nc.scalar

            def power(g, s8, t8):
                s = s8 % U
                act.wait_ge(d_own.sem, d_own.at(g))
                a.activation(small[:, s, 0, :], small[:, s, 0, :], ACT.Exp).then_inc(d_pow.sem, 1)

            def normed(g, s8, t8):
                s = s8 % U
                if started(g, 2):
                    act.wait_ge(d_up.sem, d_up.at(g - 2))
                norm_apply(act, d_norm1, g, s, mix[:, s % 2, :, :], ring_z[:, s, :, :], d_nrm)

            def copy(g, s, t):
                act.wait_ge(d_up.sem, d_up.at(g))
                if started(g, 2):
                    act.wait_ge(d_hid.sem, d_hid.at(g - 2))
                a.activation(feat[0][:, s % 2, :, :].rearrange("p h n -> p (h n)"), bank[2 + s % 2][:, :],
                             ACT.Copy).then_inc(d_feat.sem, 1)

            def relu(g, s, t):
                act.wait_ge(d_hid.sem, d_hid.at(g))
                if started(g, 2):
                    act.wait_ge(d_mul.sem, d_mul.at(g - 2))
                for f in range(2):
                    last = a.activation(hid[:, s % 2, f, :], bank[4 + s % 2][:, f * D:(f + 1) * D], ACT.Relu,
                                        bias=m1_col[:, f:f + 1])
                last.then_inc(d_relu.sem, 1)

            def result(g, s8, t8):
                s = s8 % U
                if started(g):
                    act.wait_ge(stored[s], stores(3, round_u(g, s8, t8) - 1))
                norm_apply(act, d_norm2, g, s, ring_o[:, s, :, :], mlp_z[:, s % 2, :, :], d_out)

            def roots1(g, s, t):
                norm_roots(act, d_norm1, g, s % U)

            def roots2(g, s, t):
                norm_roots(act, d_norm2, g, s % U)
            rounds(act, NG, [(4, normed), (8, result), (5, relu), (7, roots2), (3, roots1), (4, copy),
                             (0, power)], RA)

        mlp_z = feat[1][:, :, :, :].rearrange("p s h n -> p s (h n)").rearrange("p s (j d) -> p s j d", j=J)

        e_up = Count(sem("e_up"))
        e_feat = Count(sem("e_feat"))
        e_mul = Count(sem("e_mul"))
        e_plus = Count(sem("e_plus"))
        e_res = Count(sem("e_res"))
        e_out = Count(sem("e_out"))
        e_norm = norm_counts("e_norm")

        def gcn_sync(sp):
            def load(g, s, t):
                if started(g):
                    sp.wait_ge(e_res.sem, e_res.at(g - U))
                    sp.sem_inc(held, 1)
                    sp.wait_ge(e_up.sem, e_up.at(g - U))
                    sp.sem_inc(held, 1)
                fetch(sp, x3, g, ring_a, s, loaded[s])
                fetch(sp, sums_src, g, ring_s, s, loaded[s])

            def store(g, s, t):
                sp.wait_ge(e_out.sem, e_out.at(g))
                sp.sem_inc(held, 1)
                put_out(sp, out, g, ring_o, s, stored[s])

            sums_complete(sp, 4)
            rounds(sp, NG, [(0, load), (7, store)], U, peel=True)
            step_complete(sp, 4)

        def gcn_dve(dve):
            v = nc.vector

            def residual(g, s, t, k):
                z = ring_z[:, s, :, :]
                if k == 0:
                    dve.wait_ge(e_mul.sem, e_mul.at(g))
                    dve.wait_ge(e_plus.sem, e_plus.at(g))
                    if started(g):
                        dve.wait_ge(e_out.sem, e_out.at(g - U))
                    v.tensor_tensor(z, psum2(4 + s % 2), ring_a[:, s, :, :], ALU.add).then_inc(e_res.sem, 1)
                else:
                    if k == 1:
                        dve.wait_ge(e_res.sem, e_res.at(g))
                    norm_stats(dve, e_norm, g, s, z, k - 1)

            def refine_and_residual(fix, res):
                for k in range(4):
                    if fix:
                        norm_refine(dve, e_norm, *fix[:2], k)
                    if res:
                        residual(*res, k)
            rounds(dve, NG, [((4, 2), refine_and_residual)])

        def gcn_pool(pool):
            def plus(g, s, t):
                pool.wait_ge(loaded[s], loads(4, t))
                nc.gpsimd.tensor_tensor(ring_a[:, s, :, :], ring_a[:, s, :, :], row2(l3_row), ALU.add
                                        ).then_inc(e_plus.sem, 1)
            rounds(pool, NG, [(0, plus)])

        def gcn_pe(pe):
            def up_(g, s, t):
                pe.wait_ge(loaded[s], loads(4, t))
                if started(g, 2):
                    pe.wait_ge(e_feat.sem, e_feat.at(g - 2))
                turn_rows(ring_s[:, s, :, 0:D], bank[2 + s % 2]).then_inc(e_up.sem, 1)

            def mul(g, s, t):
                pe.wait_ge(e_feat.sem, e_feat.at(g))
                if started(g, 2):
                    pe.wait_ge(e_res.sem, e_res.at(g - 2))
                times(bank[4 + s % 2], [(feat[0][:, s % 2, :, :], w_l3)]).then_inc(e_mul.sem, 1)
            rounds(pe, NG, [(0, up_), (1, mul)])

        def gcn_act(act):
            def copy(g, s, t):
                act.wait_ge(e_up.sem, e_up.at(g))
                if started(g, 2):
                    act.wait_ge(e_mul.sem, e_mul.at(g - 2))
                nc.scalar.activation(feat[0][:, s % 2, :, :].rearrange("p h n -> p (h n)"), bank[2 + s % 2][:, :],
                                     ACT.Copy).then_inc(e_feat.sem, 1)

            def result(g, s, t):
                if started(g):
                    act.wait_ge(stored[s], stores(4, t - 1))
                norm_apply(act, e_norm, g, s, ring_o[:, s, :, :], ring_z[:, s, :, :], e_out)

            def roots(g, s, t):
                norm_roots(act, e_norm, g, s)
            rounds(act, NG, [(0, copy), (2, roots), (4, result)])

        block = ctx.enter_context(nc.Block())

        @block.sync
        def _(sp):
            weights_sync(sp)
            sort_sync(sp)
            sp.sem_inc(tables_done, 1)
            hop_sync(sp)
            sgc_sync(sp)
            sage_sync(sp)
            gat_sync(sp)
            gcn_sync(sp)

        @block.gpsimd
        def _(pool):
            sort_pool(pool)
            for run in range(RUNS):
                if run == 3:
                    attention_pool(pool)
                edges_pool(pool, run)
                if run == 1:
                    sgc_pool(pool)
                if run == 3:
                    gat_pool(pool)
            gcn_pool(pool)

        @block.vector
        def _(dve):
            nc.vector.memset(zero_w[:, :], 0.0).then_inc(zero_w_made, 1)
            sort_dve(dve)
            weights_vec(dve)
            for run, nodes in enumerate((hop_dve, sgc_dve, sage_dve, gat_dve, gcn_dve)):
                if run == 3:
                    attention_dve(dve)
                if run == 4:
                    make_same(dve, 1)
                edges_dve(dve, run)
                nodes(dve)

        @block.tensor
        def _(pe):
            sort_pe(pe)
            weights_tensor(pe)
            for run, nodes in enumerate((None, sgc_pe, sage_pe, gat_pe, gcn_pe)):
                if run == 3:
                    attention_pe(pe)
                if run == 4:
                    make_same_pe(pe, 1)
                edges_pe(pe, run)
                if nodes:
                    nodes(pe)

        @block.scalar
        def _(act):
            act.preload_act_table_set("natural_log_exp_and_others")
            act.wait_ge(zero_w_made, 1)
            sort_act(act)
            for run, nodes in enumerate((hop_act, sgc_act, sage_act, gat_act, gcn_act)):
                if run == 3:
                    attention_act(act)
                edges_act(act, run)
                nodes(act)


_INS = ['x', 'src', 'dst', 'edge_weight', 'L0_gnn_W', 'L0_gnn_b', 'L1_gnn_W_self', 'L1_gnn_W_neigh', 'L1_gnn_b',
        'L2_gnn_W', 'L2_gnn_att_src', 'L2_gnn_att_dst', 'L2_gnn_bias', 'L2_gnn_ln_g', 'L2_gnn_ln_b',
        'L2_gnn_W1', 'L2_gnn_b1', 'L2_gnn_W2', 'L2_gnn_b2', 'L3_gnn_weight', 'L3_gnn_bias']


def kernel(**inputs):
    import numpy as _np
    import concourse.bacc as _bacc
    from concourse import mybir as _mybir
    from concourse.bass_utils import run_bass_kernel_spmd as _run

    nc = _bacc.Bacc("TRN2", target_bir_lowering=False, num_devices=1)
    arrays, args = {}, []
    for name in _INS:
        a = _np.ascontiguousarray(inputs[name])
        arrays[f"in_{name}_dram"] = a
        args.append(nc.dram_tensor(f"in_{name}_dram", a.shape, _mybir.dt.from_np(a.dtype), kind="ExternalInput").ap())
    out = nc.dram_tensor("out_0_dram", (50000, 256), _mybir.dt.float32, kind="ExternalOutput").ap()
    gnn_program(nc, *args, out)
    r = _run(nc, [arrays], core_ids=[0])
    return r.results[0]["out_0_dram"]
```
